# Optimizing a Trainium2 kernel written in Bass

```python
import numpy as np
import jax
import jax.numpy as jnp

def _softmax(x, axis=-1):
    return jax.nn.softmax(x, axis=axis)

def _gelu(x):
    return jax.nn.gelu(x, approximate=True)

def _silu(x):
    return jax.nn.silu(x)

def _sigmoid(x):
    return jax.nn.sigmoid(x)

def _layernorm(x, axis=-1, eps=1e-05):
    m = jnp.mean(x, axis=axis, keepdims=True)
    v = jnp.var(x, axis=axis, keepdims=True)
    return (x - m) / jnp.sqrt(v + eps)

def _scatter_add(tgt, idx, src, axis=0):
    return tgt.at[idx].add(src)

def _segment_sum(src, seg, n):
    return jax.ops.segment_sum(src, seg, n)
kernel_name = 'mk_sandwich_d1_jaxref_r8_592bdd'

def setup_inputs(seed: int=0):
    np.random.seed(seed)
    _w = jnp.asarray

    def _L0_attn_setup():
        import jax, jax.numpy as jnp
        import numpy as np
        import math
        D_MODEL = 128
        LN_EPS = 1e-05

        def _layer_norm(x):
            mu = jnp.mean(x, axis=-1, keepdims=True)
            var = jnp.var(x, axis=-1, keepdims=True)
            return (x - mu) * jax.lax.rsqrt(var + LN_EPS)
        key = jax.random.key(seed)
        ks = jax.random.split(key, 5)
        B, S, D = (4, 256, D_MODEL)
        scale = 1.0 / math.sqrt(D)
        x = jax.random.normal(ks[0], (B, S, D), dtype=jnp.float32)
        Wq = jax.random.normal(ks[1], (D, D), dtype=jnp.float32) * scale
        Wk = jax.random.normal(ks[2], (D, D), dtype=jnp.float32) * scale
        Wv = jax.random.normal(ks[3], (D, D), dtype=jnp.float32) * scale
        Wo = jax.random.normal(ks[4], (D, D), dtype=jnp.float32) * scale
        b = jnp.zeros((D,), dtype=jnp.float32)
        layerscale = 0.0001 * jnp.ones((D,), dtype=jnp.float32)
        return {'x': x, 'Wq': Wq, 'bq': b, 'Wk': Wk, 'bk': b, 'Wv': Wv, 'bv': b, 'Wo': Wo, 'bo': b, 'layerscale': layerscale}
    _L0_attn_in = _L0_attn_setup()

    def _L0_ffn_setup():
        import jax, jax.numpy as jnp
        import numpy as np
        B, S, H, E, K, I = (4, 256, 128, 8, 2, 512)
        GATE_EPS = 1e-06
        LN_EPS = 1e-05
        key = jax.random.key(seed)
        k0, k1, k2, k3 = jax.random.split(key, 4)
        x = jax.random.normal(k0, (B, S, H), jnp.float32)
        gate_w = jax.random.normal(k1, (E, H), jnp.float32) * np.float32(np.sqrt(2.0 / (H + E)))
        expert_bias = jnp.zeros((E,), jnp.float32)
        w_up = jax.random.normal(k2, (E, I, H), jnp.float32) * np.float32(np.sqrt(2.0 / (H + I)))
        w_down = jax.random.normal(k3, (E, H, I), jnp.float32) * np.float32(np.sqrt(2.0 / (H + I)))
        return {'x': x, 'gate_w': gate_w, 'expert_bias': expert_bias, 'w_up': w_up, 'w_down': w_down}
    _L0_ffn_in = _L0_ffn_setup()
    _d = {'L0_attn_x': _L0_attn_in['x'], 'L0_attn_Wq': _L0_attn_in['Wq'], 'L0_attn_bq': _L0_attn_in['bq'], 'L0_attn_Wk': _L0_attn_in['Wk'], 'L0_attn_bk': _L0_attn_in['bk'], 'L0_attn_Wv': _L0_attn_in['Wv'], 'L0_attn_bv': _L0_attn_in['bv'], 'L0_attn_Wo': _L0_attn_in['Wo'], 'L0_attn_bo': _L0_attn_in['bo'], 'L0_attn_layerscale': _L0_attn_in['layerscale'], 'L0_ffn_gate_w': _L0_ffn_in['gate_w'], 'L0_ffn_expert_bias': _L0_ffn_in['expert_bias'], 'L0_ffn_w_up': _L0_ffn_in['w_up'], 'L0_ffn_w_down': _L0_ffn_in['w_down']}
    _x0 = _d['L0_attn_x']
    _d['L0_attn_x'] = jax.random.normal(jax.random.fold_in(jax.random.key(seed), 1), (4, 1024, 128), dtype=_x0.dtype)
    del _x0
    return _d

def reference(L0_attn_x, L0_attn_Wq, L0_attn_bq, L0_attn_Wk, L0_attn_bk, L0_attn_Wv, L0_attn_bv, L0_attn_Wo, L0_attn_bo, L0_attn_layerscale, L0_ffn_gate_w, L0_ffn_expert_bias, L0_ffn_w_up, L0_ffn_w_down):

    def _L0_attn_ref(x, Wq, bq, Wk, bk, Wv, bv, Wo, bo, layerscale):
        import jax, jax.numpy as jnp
        import numpy as np
        import math
        D_MODEL = 128
        LN_EPS = 1e-05

        def _layer_norm(x):
            mu = jnp.mean(x, axis=-1, keepdims=True)
            var = jnp.var(x, axis=-1, keepdims=True)
            return (x - mu) * jax.lax.rsqrt(var + LN_EPS)
        B, S, D = x.shape
        q = jnp.einsum('bsd,ed->bse', x, Wq) + bq
        k = jnp.einsum('bsd,ed->bse', x, Wk) + bk
        v = jnp.einsum('bsd,ed->bse', x, Wv) + bv
        qn = _layer_norm(q)
        kn = _layer_norm(k)
        scores = jnp.einsum('bse,bte->bst', qn, kn) / jnp.sqrt(jnp.float32(D))
        attn = jax.nn.sigmoid(scores - jnp.log(jnp.float32(S)))
        out = jnp.einsum('bst,bte->bse', attn, v)
        proj = jnp.einsum('bsd,ed->bse', out, Wo) + bo
        return proj * layerscale

    def _L0_ffn_ref(x, gate_w, expert_bias, w_up, w_down):
        import jax, jax.numpy as jnp
        import numpy as np
        B, S, H, E, K, I = (4, 256, 128, 8, 2, 512)
        GATE_EPS = 1e-06
        LN_EPS = 1e-05
        logits = jnp.einsum('bsh,eh->bse', x, gate_w) + expert_bias
        weights = jax.nn.softmax(logits, axis=-1)
        top_w, top_i = jax.lax.top_k(weights, K)
        top_w = top_w / (jnp.sum(top_w, axis=-1, keepdims=True) + GATE_EPS)
        sparse_w = jnp.sum(jax.nn.one_hot(top_i, E, dtype=weights.dtype) * top_w[..., None], axis=-2)
        out = jnp.zeros_like(x)
        for e in range(E):
            h = jax.nn.gelu(jnp.einsum('bsh,ih->bsi', x, w_up[e]), approximate=False)
            y = jnp.einsum('bsi,hi->bsh', h, w_down[e])
            out = out + sparse_w[..., e:e + 1] * y
        mu = jnp.mean(out, axis=-1, keepdims=True)
        var = jnp.mean(jnp.square(out - mu), axis=-1, keepdims=True)
        out = (out - mu) * jax.lax.rsqrt(var + LN_EPS)
        return out + x
    x = L0_attn_x
    x = x + _layernorm(_L0_attn_ref(_layernorm(x, axis=-1), L0_attn_Wq, L0_attn_bq, L0_attn_Wk, L0_attn_bk, L0_attn_Wv, L0_attn_bv, L0_attn_Wo, L0_attn_bo, L0_attn_layerscale), axis=-1)
    x = x + _layernorm(_L0_ffn_ref(_layernorm(x, axis=-1), L0_ffn_gate_w, L0_ffn_expert_bias, L0_ffn_w_up, L0_ffn_w_down), axis=-1)
    return x

_drawn_inputs = setup_inputs


def setup_inputs(seed=0):
    import zlib

    import numpy as np

    out = dict(_drawn_inputs(seed))
    spreads = {'L0_attn_bq': (0.0, 0.8),
     'L0_attn_bk': (0.0, 0.8),
     'L0_attn_bv': (0.0, 0.344),
     'L0_attn_bo': (0.0, 0.615),
     'L0_attn_layerscale': (9.999999747378752e-05, 0.6),
     'L0_ffn_expert_bias': (0.0, 0.1)}
    factors = {'L0_attn_Wq': 3.2, 'L0_attn_Wk': 3.131, 'L0_attn_Wv': 3.313, 'L0_attn_Wo': 2.683}
    for name, (base, spread) in spreads.items():
        noise = np.random.default_rng([zlib.crc32(name.encode()), seed]).standard_normal(out[name].shape)
        drawn = base * np.exp(spread * noise) if base else spread * noise
        out[name] = jnp.asarray(drawn.astype(out[name].dtype))
    for name, factor in factors.items():
        out[name] = (out[name] * factor).astype(out[name].dtype)
    return out
```

```python
from contextlib import ExitStack

import numpy as np

import concourse.bass as bass
from concourse import mybir

F32 = mybir.dt.float32
F32R = mybir.dt.float32r
I32 = mybir.dt.int32
U32 = mybir.dt.uint32
ALU = mybir.AluOpType
ACT = mybir.ActivationFunctionType
AX = mybir.AxisListType

P = 128
LN_EPS = 1e-5
GATE_EPS = 1e-6


class Count:

    def __init__(self, sem):
        self.sem, self.n = sem, 0

    def up(self, ins):
        self.n += 1
        ins.then_inc(self.sem, 1)

    def settle(self, eng, ins):
        self.up(ins)
        eng.wait_ge(self.sem, self.n)


def build_program(nc, x, Wq, bq, Wk, bk, Wv, bv, Wo, bo, layerscale, gate_w, expert_bias, w_up, w_down, out):
    B, S, D = x.shape
    E, I, _ = w_up.shape
    assert D == P and S % 512 == 0 and I == 512
    BT = S // P
    NT = B * BT
    HALVES = 2
    HT = NT // HALVES
    HB = B // HALVES
    TOPK = 2
    FT = (HT * P * TOPK + E * (P - 1)) // P
    LOOPS = (FT - 4) // 2
    AHEAD = 6
    IC = I // P
    QG = S // 512
    GT = 512 // P
    LOG_S = float(np.log(np.float32(S)))
    K_SCALE = float(1.0 / np.sqrt(np.float32(D)))

    xs = [nc.dram_tensor(f"sorted_x{h}", [FT * P, D], F32, kind="Internal").ap() for h in range(HALVES)]
    ys = [nc.dram_tensor(f"sorted_y{h}", [FT * P, D], F32, kind="Internal").ap() for h in range(HALVES)]

    x_t = x.rearrange("b (t p) d -> p (b t) d", p=P)
    out_t = out.rearrange("b (t p) d -> p (b t) d", p=P)

    with ExitStack() as ctx:
        def sb(name, shape, dt=F32):
            return ctx.enter_context(nc.sbuf_tensor(name, shape, dt))

        def sem(name):
            return ctx.enter_context(nc.semaphore(name))

        X = sb("X", [P, NT, D])
        XN2 = sb("XN2", [P, NT, D])
        wup_hi = sb("wup_hi", [P, E * I], F32R)
        wup_lo = sb("wup_lo", [P, E * I], F32R)
        wdn = sb("wdn", [P, E * IC * 2 * D], F32R)
        stage_up = sb("stage_up", [P, 2, IC, P])
        stage_dn = sb("stage_dn", [P, 2, I])
        wnat = sb("wnat", [P, 4, P])
        w_qkv = sb("w_qkv", [P, 3 * P])
        w_o = sb("w_o", [P, P])
        b_row = sb("b_row", [P, 6, P])
        wsum = sb("wsum", [P, 8])
        gate_nat = sb("gate_nat", [E, P])
        gate_T = sb("gate_T", [P, E])
        eb_row = sb("eb_row", [P, E])
        ident = sb("ident", [P, P])
        ones = sb("ones", [P, P])
        before = sb("before", [P, P])
        zeros = sb("zeros", [P, 2, D])
        neg_log_s = sb("neg_log_s", [P, 1])
        xn = sb("xn", [P, BT, D])
        xnT = sb("xnT", [P, S])
        kT_hi = sb("kT_hi", [P, 2, S], F32R)
        kT_lo = sb("kT_lo", [P, 2, S], F32R)
        qT_hi = sb("qT_hi", [P, 2, S], F32R)
        qT_lo = sb("qT_lo", [P, 2, S], F32R)
        QK = sb("QK", [P, BT, 2, P])
        V = sb("V", [P, 2, BT, D])
        probs = sb("probs", [P, 2, S])
        oT = sb("oT", [P, S])
        proj = sb("proj", [P, BT, D])
        xn2T = xnT
        scrap = sb("scrap", [P, P])
        L = sb("L", [P, NT, E])
        bst = sb("bst", [P, BT, 6])
        mv_x = sb("mv_x", [P, BT, 2])
        mv_n = sb("mv_n", [P, BT, 2])
        ss_qk = sb("ss_qk", [P, 2, BT])
        ss_p = sb("ss_p", [P, BT])
        r_x = sb("r_x", [P, BT])
        r_qk = sb("r_qk", [P, 2, BT])
        r_p = sb("r_p", [P, BT])
        r_n = sb("r_n", [P, BT])
        nv, nh, ntm = (sb(n, [P, 2 * BT]) for n in ("newton_v", "newton_h", "newton_t"))
        desc = sb("desc", [P, E])
        seg = sb("seg", [P, E * HT])
        thr = sb("thr", [P, HT])
        tix = sb("tix", [P, FT])
        m1 = sb("m1", [P, HT])
        m2 = sb("m2", [P, HT])
        kk = sb("kk", [P, HT])
        oh = [sb(f"oh{k}", [P, HT, E]) for k in range(TOPK)]
        ra = sb("ra", [P, HT, E])
        rb = sb("rb", [P, HT, E])
        ED = sb("ED", [P, HT, E + 1])
        zs = sb("zs", [P, HT])
        chosen = sb("chosen", [P, HT, E])
        incl = sb("incl", [P, E, HT])
        tot = sb("tot", [P, E, HT])
        gtt = sb("gtt", [P, E, HT])
        ntile = sb("ntile", [P, E])
        endt = sb("endt", [P, E])
        base = sb("base", [P, E])
        ext = sb("ext", [P, FT, E])
        exf = sb("exf", [P, FT])
        exp_packed = sb("exp_packed", [P, FT])
        experts = sb("experts", [P, HALVES, FT], I32)
        gates = sb("gates", [P, HALVES, TOPK, HT])
        slots_f = sb("slots_f", [P, HT])
        slots = sb("slots", [P, HALVES, TOPK, HT], U32)
        xin = sb("xin", [P, 2, D])
        xT_hi = sb("xT_hi", [P, 2, P], F32R)
        xT_lo = sb("xT_lo", [P, 2, P], F32R)
        hid = probs[:, 0, :].rearrange("p (a i) -> p a i", a=2)
        hT_hi = kT_hi[:, 0, :].rearrange("p (a i) -> p a i", a=2)
        hT_lo = kT_lo[:, 0, :].rearrange("p (a i) -> p a i", a=2)
        yo = sb("yo", [P, 2, D])
        G = [QK, V[:, :, :, :].rearrange("p a t d -> p (a t d)").rearrange("p (t k d) -> p t k d", k=TOPK, d=D)]
        fo = proj
        fz = oT[:, :].rearrange("p (t d) -> p t d", d=D)

        psS = ctx.enter_context(nc.psum_tensor("psS", [P, 2, S], F32))
        psO = ctx.enter_context(nc.psum_tensor("psO", [P, S], F32))
        psW = ctx.enter_context(nc.psum_tensor("psW", [P, 2, 512], F32))
        psU = psS[:, 0, :].rearrange("p (a n) -> p a n", a=2)
        psH = psS[:, 1, :].rearrange("p (a n) -> p a n", a=2)
        psX = psO[:, :].rearrange("p (a n) -> p a n", a=2)
        psY = psW

        x_loaded = [sem(f"x_loaded{b}") for b in range(B)]
        w_loaded = sem("w_loaded")
        row_loaded = sem("row_loaded")
        up_loaded = [sem(f"up_loaded{i}") for i in range(2)]
        dn_loaded = [sem(f"dn_loaded{i}") for i in range(2)]
        cleared = sem("cleared")
        consts = sem("consts")
        dve_consts = sem("dve_consts")
        weights_ready = sem("weights_ready")
        step_done = sem("step_done")
        act_drained = sem("act_drained")
        dve_drained = sem("dve_drained")
        scores_done = sem("scores_done")
        probs_ready = sem("probs_ready")
        pv_done = sem("pv_done")
        oT_ready = sem("oT_ready")
        x_stats = sem("x_stats")
        rx_ready = sem("rx_ready")
        rn_ready = sem("rn_ready")
        xn_ready = sem("xn_ready")
        qk_stats = sem("qk_stats")
        rk_ready = sem("rk_ready")
        qs_ready = sem("qs_ready")
        ks_ready = sem("ks_ready")
        p_stats = sem("p_stats")
        rp_ready = sem("rp_ready")
        n_stats = sem("n_stats")
        xn2_ready = sem("xn2_ready")
        exp_in = sem("exp_in")
        exp_out = sem("exp_out")
        chosen_ready = sem("chosen_ready")
        routed = sem("routed")
        scattered = [sem(f"scattered{h}") for h in range(HALVES)]
        xin_loaded = [sem(f"xin_loaded{i}") for i in range(2)]
        xT_done = sem("xT_done")
        xhi_ready = sem("xhi_ready")
        xlo_ready = sem("xlo_ready")
        up_done = sem("up_done")
        hid_ready = sem("hid_ready")
        hT_done = sem("hT_done")
        hhi_ready = sem("hhi_ready")
        hlo_ready = sem("hlo_ready")
        down_done = sem("down_done")
        yo_ready = sem("yo_ready")
        y_stored = [sem(f"y_stored{i}") for i in range(2)]
        gathered = [sem(f"gathered{g}") for g in range(NT // BT)]
        mixed0 = sem("mixed0")
        f_in = sem("f_in")
        f_norm = sem("f_norm")
        g_free = sem("g_free")
        final_ready = sem("final_ready")
        stored = [sem(f"stored{g}") for g in range(NT // BT)]
        s_dve, s_act, s_pool = sem("dve_own"), sem("act_own"), sem("pool_own")

        def front(b):
            return {0: [("xT", b, 0), ("xT", b, 1)],
                    1: [("qkv", b, 0), ("qkv", b, 1)], 2: [("qkv", b, 2), ("qkv", b, 3)],
                    3: [("qkv", b, 4), ("qkv", b, 5)], 4: [("qkv", b, 6), ("qkv", b, 7)],
                    6: [("qT", b, 0), ("kT", b, 0)], 7: [("qT", b, 1), ("kT", b, 1)]}

        def back(b):
            return {2: [("pj", b, 0), ("pj", b, 1)], 5: [("nT", b, 0), ("nT", b, 1)], 6: [("lg", b, 0)]}

        def weights_of(J):
            e, odd = J // 4, J % 4
            return [("wu", e, 0)] if odd == 1 else [("wd", e, 0)] if odd == 3 else []

        plan = [("setup", -1, s) for s in (("wa", 0, 0), ("gt", 0, 0))]
        for s in range(8):
            plan += [("step", -1, st) for st in front(0).get(s, [])]
        NJ = B * BT
        for J in range(NJ):
            b, j = divmod(J, BT)
            plan.append(("scores", J, None))
            if b > 0:
                plan += [("step", J, st) for st in back(b - 1).get(j, [])]
            if b + 1 < B:
                plan += [("step", J, st) for st in front(b + 1).get(j, [])]
            plan += [("step", J, st) for st in weights_of(J)]
            if b > HB and (b - 1) % HB == 0 and j == 1:
                plan.append(("step", J, ("rt", (b - 1) // HB - 1, 0)))
            if J > 0:
                plan.append(("pv", J - 1, None))
        plan.append(("pv", NJ - 1, None))
        for s in range(8):
            plan += [("step", NJ, st) for st in back(B - 1).get(s, [])]
        plan.append(("step", NJ, ("rt", HALVES - 1, 0)))

        READERS = {"wa": "V", "gt": "V", "xT": "A", "qkv": "V", "qT": "AV", "kT": "AV", "pj": "V",
                   "nT": "A", "lg": "V", "wu": "AV", "wd": "AV", "rt": "V"}
        steps = [s for _, _, s in plan if s is not None]
        number = {s: n for n, s in enumerate(steps)}
        act_at, dve_at, na, nd = {}, {}, 0, 0
        for s in steps:
            na += "A" in READERS[s[0]]
            nd += "V" in READERS[s[0]]
            act_at[s], dve_at[s] = na, nd

        def bank(s):
            return psW[:, number[s] % 2, :]

        def wdn_parts(e):
            return wdn[:, 2 * e * I:2 * (e + 1) * I].rearrange("p (c a h) -> p c a h", a=2, h=D)

        block = ctx.enter_context(nc.Block())

        @block.sync
        def _(sp):
            sp.dma_start(X[:, 0:BT, :], x_t[:, 0:BT, :]).then_inc(x_loaded[0], 16)
            for i, w in enumerate((Wq, Wk, Wv, Wo)):
                sp.dma_start(wnat[:, i, :], w).then_inc(w_loaded, 16)
            for i, r in enumerate((bq, bk, bv, bo, layerscale)):
                sp.dma_start(b_row[:, i, :], r.rearrange("(a d) -> a d", a=1).to_broadcast([P, D])).then_inc(row_loaded, 16)
            sp.dma_start(eb_row[:, :], expert_bias.rearrange("(a d) -> a d", a=1).to_broadcast([P, E])).then_inc(row_loaded, 16)
            sp.dma_start(gate_nat[:, :], gate_w).then_inc(w_loaded, 16)
            for b in range(1, B):
                sp.dma_start(X[:, b * BT:(b + 1) * BT, :], x_t[:, b * BT:(b + 1) * BT, :]).then_inc(x_loaded[b], 16)
            sp.wait_ge(consts, 4)
            for h in range(HALVES):
                sp.dma_start(xs[h].rearrange("(p r) d -> p r d", p=P), zeros[:, 0:1, :].to_broadcast([P, FT, D])).then_inc(cleared, 16)
            for e in range(E):
                if e >= 2:
                    sp.wait_ge(step_done, number[("wd", e - 2, 0)] + 1)
                sp.dma_start(stage_up[:, e % 2, :, :], w_up[e].rearrange("(c p) h -> p c h", p=P)).then_inc(up_loaded[e % 2], 16)
                sp.dma_start(stage_dn[:, e % 2, :], w_down[e]).then_inc(dn_loaded[e % 2], 16)

            for h in range(HALVES):
                t0 = h * FT
                sp.wait_ge(scattered[h], 16 * HT * TOPK)
                for i in range(AHEAD):
                    if t0 + i >= 2:
                        sp.wait_ge(xT_done, t0 + i - 1)
                    sp.dma_start(xin[:, (t0 + i) % 2, :], xs[h][i * P:(i + 1) * P, :]).then_inc(xin_loaded[(t0 + i) % 2], 16)
                PAIRS = (FT - AHEAD) // 2
                with sp.Fori(0, PAIRS) as k:
                    for u in range(2):
                        sp.wait_ge(yo_ready, k * 2 + (t0 + u + 1))
                        sp.dma_start(ys[h][bass.ds(k * (2 * P) + u * P, P), :], yo[:, (t0 + u) % 2, :]).then_inc(y_stored[(t0 + u) % 2], 16)
                        sp.wait_ge(xT_done, k * 2 + (t0 + u + AHEAD - 1))
                        sp.dma_start(xin[:, (t0 + u + AHEAD) % 2, :], xs[h][bass.ds(k * (2 * P) + (u + AHEAD) * P, P), :]
                                     ).then_inc(xin_loaded[(t0 + u + AHEAD) % 2], 16)
                for i in range(2 * PAIRS, FT):
                    sp.wait_ge(yo_ready, t0 + i + 1)
                    sp.dma_start(ys[h][i * P:(i + 1) * P, :], yo[:, (t0 + i) % 2, :]).then_inc(y_stored[(t0 + i) % 2], 16)
                    if i + AHEAD < FT:
                        sp.wait_ge(xT_done, t0 + i + AHEAD - 1)
                        sp.dma_start(xin[:, (t0 + i + AHEAD) % 2, :], xs[h][(i + AHEAD) * P:(i + AHEAD + 1) * P, :]
                                     ).then_inc(xin_loaded[(t0 + i + AHEAD) % 2], 16)
            for g in range(NT // BT):
                sp.wait_ge(final_ready, g + 1)
                sp.dma_start(out_t[:, g * BT:(g + 1) * BT, :], fz[:, :, :] if g % 2 == 0 else xn[:, :, :]).then_inc(stored[g], 16)
            for g in range(NT // BT):
                sp.wait_ge(stored[g], 16)

        @block.gpsimd
        def _(pool):
            own = Count(s_pool)
            own.settle(pool, pool.memset(ident[:, :], 0.0))
            pool.affine_select(out=ident[:, :], in_=ident[:, :], compare_op=ALU.not_equal, fill=1.0, base=0,
                               pattern=[[-1, P]], channel_multiplier=1).then_inc(consts, 1)
            pool.memset(zeros[:, :, :], 0.0).then_inc(consts, 1)
            own.settle(pool, pool.memset(ones[:, :], 1.0))
            pool.affine_select(out=before[:, :], in_=ones[:, :], compare_op=ALU.is_gt, fill=0.0, base=0,
                               pattern=[[1, P]], channel_multiplier=-1).then_inc(consts, 1)
            pool.memset(neg_log_s[:, :], -LOG_S).then_inc(consts, 1)
            for e in range(E):
                pool.memset(desc[:, e:e + 1], float(E - e))
            pool.memset(seg[:, :], 1.0)
            own.settle(pool, pool.iota(tix[:, :], pattern=[[1, FT]], base=0, channel_multiplier=0, allow_small_or_imprecise_dtypes=True))
            own.settle(pool, pool.tensor_scalar(thr[:, :], tix[:, 0:HT], float(P), None, ALU.mult))
            pool.memset(seg[:, :].rearrange("p (e t) -> p e t", t=HT)[:, :, 0:1], 0.0).then_inc(consts, 1)

            def rsqrt(dst, src, scale, n):
                own.settle(pool, pool.tensor_scalar(nv[:, 0:n], src, scale, LN_EPS, ALU.mult, ALU.add))
                own.settle(pool, pool.tensor_scalar(dst.bitcast(I32), nv[:, 0:n].bitcast(I32), -0.5, float(0x5f3759df), ALU.mult, ALU.add))
                own.settle(pool, pool.tensor_scalar(nh[:, 0:n], nv[:, 0:n], -0.5, None, ALU.mult))
                for _ in range(3):
                    own.settle(pool, pool.tensor_tensor(ntm[:, 0:n], dst, nh[:, 0:n], ALU.mult))
                    own.settle(pool, pool.tensor_tensor(ntm[:, 0:n], dst, ntm[:, 0:n], ALU.mult))
                    own.settle(pool, pool.tensor_scalar(ntm[:, 0:n], ntm[:, 0:n], 1.5, None, ALU.add))
                    own.settle(pool, pool.tensor_tensor(dst, dst, ntm[:, 0:n], ALU.mult))

            def norm_x(b):
                pool.wait_ge(x_stats, b + 1)
                rsqrt(r_x[:, :], mv_x[:, :, 1], 1.0, BT)
                pool.engine_nop().then_inc(rx_ready, 1)

            def norm_qk(b):
                pool.wait_ge(qk_stats, b + 1)
                rsqrt(r_qk[:, :, :].rearrange("p a t -> p (a t)"), ss_qk[:, :, :].rearrange("p a t -> p (a t)"), 1.0 / D, 2 * BT)
                pool.engine_nop().then_inc(rk_ready, 1)

            def norm_p(b):
                pool.wait_ge(p_stats, b + 1)
                rsqrt(r_p[:, :], ss_p[:, :], 1.0 / D, BT)
                pool.engine_nop().then_inc(rp_ready, 1)

            def norm_n(b):
                pool.wait_ge(n_stats, b + 1)
                rsqrt(r_n[:, :], mv_n[:, :, 1], 1.0, BT)
                pool.engine_nop().then_inc(rn_ready, 1)

            def scatter(h, t_from, t_to):
                if t_from == 0:
                    if h == 0:
                        pool.wait_ge(cleared, 16 * HALVES)
                    pool.wait_ge(xn2_ready, (h + 1) * HB)
                    pool.wait_ge(routed, h + 1)
                for t in range(t_from, t_to):
                    for k in range(TOPK):
                        pool.indirect_dma_start(xs[h][:, :], bass.IndirectOffsetOnAxis(ap=slots[:, h, k, t:t + 1], axis=0),
                                                XN2[:, h * HT + t, :], None).then_inc(scattered[h], 16)

            def gather(g):
                h = g * BT // HT
                if g * BT % HT == 0:
                    last = (h + 1) * FT
                    pool.wait_ge(y_stored[0], 16 * ((last + 1) // 2))
                    pool.wait_ge(y_stored[1], 16 * (last // 2))
                if g >= 2:
                    pool.wait_ge(g_free, g - 1)
                for t in range(BT):
                    for k in range(TOPK):
                        pool.indirect_dma_start(G[g % 2][:, t, k, :], None, ys[h][:, :],
                                                bass.IndirectOffsetOnAxis(ap=slots[:, h, k, g * BT % HT + t:g * BT % HT + t + 1], axis=0)
                                                ).then_inc(gathered[g], 16)

            norm_x(0)
            norm_x(1)
            norm_qk(0)
            for b in range(B):
                if b > 0:
                    norm_p(b - 1)
                if b == B - 1:
                    scatter(0, 0, 3)
                if b + 1 < B:
                    norm_qk(b + 1)
                if b > 0:
                    norm_n(b - 1)
                if b + 2 < B:
                    norm_x(b + 2)
                if b == B - 1:
                    scatter(0, 3, HT)
            norm_p(B - 1)
            norm_n(B - 1)
            scatter(1, 0, HT)
            for g in range(NT // BT):
                gather(g)

        @block.scalar
        def _(act):
            own = Count(s_act)

            def act_step(s):
                kind, b, g = s
                W = bank(s)
                if "A" not in READERS[kind]:
                    return
                act.wait_ge(step_done, number[s] + 1)
                cols = slice(g * 512, (g + 1) * 512)
                if kind == "xT":
                    act.activation(xnT[:, cols], W, ACT.Copy).then_inc(act_drained, 1)
                elif kind == "qT":
                    act.activation(qT_hi[:, b % 2, cols], W, ACT.Copy).then_inc(act_drained, 1)
                elif kind == "kT":
                    act.activation(kT_hi[:, b % 2, cols], W, ACT.Copy).then_inc(act_drained, 1)
                elif kind == "nT":
                    act.activation(xn2T[:, cols], W, ACT.Copy).then_inc(act_drained, 1)
                elif kind == "wu":
                    act.activation(wup_hi[:, b * I:(b + 1) * I], W, ACT.Copy).then_inc(act_drained, 1)
                elif kind == "wd":
                    act.activation(wdn_parts(b)[:, :, 0, :], W.rearrange("p (c h) -> p c h", h=D), ACT.Copy).then_inc(act_drained, 1)

            def route_exp(h):
                act.wait_ge(exp_in, h + 1)
                act.activation(ED[:, :, :], ED[:, :, :], ACT.Exp).then_inc(exp_out, 1)

            def scale_q(b):
                act.wait_ge(rk_ready, b + 1)
                for t in range(BT):
                    ins = act.activation(QK[:, t, 0, :], QK[:, t, 0, :], ACT.Copy, scale=r_qk[:, 0, t:t + 1])
                ins.then_inc(qs_ready, 1)

            for what, J, s in plan:
                if s is not None and s[0] == "qT" and s[2] == 0:
                    scale_q(s[1])
                if what == "scores":
                    b, j = divmod(J, BT)
                    if J == 0:
                        act.wait_ge(consts, 4)
                    act.wait_ge(scores_done, J + 1)
                    if J >= 2:
                        act.wait_ge(pv_done, J - 1)
                    act.activation(probs[:, J % 2, :], psS[:, J % 2, :], ACT.Sigmoid, bias=neg_log_s[:, 0:1],
                                   scale=K_SCALE).then_inc(probs_ready, 1)
                elif what == "pv":
                    if J % BT == BT - 1:
                        act.wait_ge(pv_done, J + 1)
                        if J // BT > 0:
                            act.wait_ge(step_done, number[("pj", J // BT - 1, 1)] + 1)
                        act.activation(oT[:, :], psO[:, :], ACT.Copy).then_inc(oT_ready, 1)
                elif s[0] == "rt":
                    route_exp(s[1])
                else:
                    act_step(s)

            def gelu(par, wait):
                act.wait_ge(up_done, wait)
                act.activation(hid[:, par, :], psU[:, par, :], ACT.Gelu).then_inc(hid_ready, 1)

            def split_hi(par, wait):
                act.wait_ge(xT_done, wait)
                act.activation(xT_hi[:, par, :], psX[:, par, 0:P], ACT.Copy).then_inc(xhi_ready, 1)

            def split_h(par, wait):
                act.wait_ge(hT_done, wait)
                act.activation(hT_hi[:, par, :], psH[:, par, :], ACT.Copy).then_inc(hhi_ready, 1)

            for h in range(HALVES):
                t0 = h * FT
                split_hi(t0 % 2, t0 + 1)
                split_hi((t0 + 1) % 2, t0 + 2)
                gelu(t0 % 2, t0 + 1)
                split_hi(t0 % 2, t0 + 3)
                gelu((t0 + 1) % 2, t0 + 2)
                split_hi((t0 + 1) % 2, t0 + 4)
                split_h(t0 % 2, t0 + 1)
                with act.Fori(0, LOOPS) as k:
                    for u in range(2):
                        gelu((t0 + u) % 2, k * 2 + (t0 + u + 3))
                        split_hi((t0 + u) % 2, k * 2 + (t0 + u + 5))
                        split_h((t0 + u + 1) % 2, k * 2 + (t0 + u + 2))
                for i in range(2 + 2 * LOOPS, FT + 1):
                    if i < FT:
                        gelu((t0 + i) % 2, t0 + i + 1)
                    if i + 2 < FT:
                        split_hi((t0 + i) % 2, t0 + i + 3)
                    split_h((t0 + i - 1) % 2, t0 + i)

            for g in range(NT // BT):
                h = g * BT // HT
                act.wait_ge(gathered[g], 16 * BT * TOPK)
                if g > 0:
                    act.wait_ge(f_in, 2 * g - 1)
                for t in range(BT):
                    ins = act.activation(fo[:, t, :], G[g % 2][:, t, 0, :], ACT.Copy, scale=gates[:, h, 0, g * BT % HT + t:g * BT % HT + t + 1])
                ins.then_inc(mixed0, 1)

        @block.tensor
        def _(pe):
            pe.wait_ge(consts, 5)

            def split3(dst, lhs, rhs, start=True, stop=True):
                pe.matmul(dst, lhs[0], rhs[0], start=True, stop=False)
                pe.matmul(dst, lhs[0], rhs[1], start=False, stop=False)
                return pe.matmul(dst, lhs[1], rhs[0], start=False, stop=True)

            def pe_step(s):
                kind, b, g = s
                W = bank(s)
                if number[s] >= 2:
                    last = steps[number[s] - 2]
                    if "A" in READERS[last[0]]:
                        pe.wait_ge(act_drained, act_at[last])
                    if "V" in READERS[last[0]]:
                        pe.wait_ge(dve_drained, dve_at[last])
                cols = slice(g * 512, (g + 1) * 512)
                if kind == "wa":
                    pe.wait_ge(w_loaded, 16 * 5)
                    for i in range(4):
                        ins = pe.transpose(W[:, i * P:(i + 1) * P], wnat[:, i, :], ident[:, :])
                elif kind == "gt":
                    ins = pe.transpose(W[:, 0:E], gate_nat[:, :], ident[0:E, 0:E])
                elif kind == "xT":
                    pe.wait_ge(xn_ready, b + 1)
                    for t in range(GT):
                        ins = pe.transpose(W[:, t * P:(t + 1) * P], xn[:, g * GT + t, :], ident[:, :])
                elif kind == "qkv":
                    if g == 0:
                        pe.wait_ge(act_drained, act_at[("xT", b, 1)])
                        if b == 0:
                            pe.wait_ge(weights_ready, 1)
                    ins = pe.matmul(W[:, 0:3 * P], xnT[:, g * P:(g + 1) * P], w_qkv[:, :], start=True, stop=True)
                elif kind in ("qT", "kT"):
                    if kind == "qT":
                        pe.wait_ge(qs_ready, b + 1)
                    else:
                        pe.wait_ge(ks_ready, b + 1)
                    for t in range(GT):
                        ins = pe.transpose(W[:, t * P:(t + 1) * P], QK[:, g * GT + t, int(kind == "kT"), :], ident[:, :])
                elif kind == "pj":
                    pe.wait_ge(oT_ready, b + 1)
                    for t in range(GT):
                        tt = g * GT + t
                        ins = pe.matmul(W[:, t * P:(t + 1) * P], oT[:, tt * P:(tt + 1) * P], w_o[:, :], start=True, stop=True)
                elif kind == "nT":
                    pe.wait_ge(xn2_ready, b + 1)
                    for t in range(GT):
                        ins = pe.transpose(W[:, t * P:(t + 1) * P], XN2[:, b * BT + g * GT + t, :], ident[:, :])
                elif kind == "lg":
                    pe.wait_ge(act_drained, act_at[("nT", b, 1)])
                    for t in range(BT):
                        ins = pe.matmul(W[:, t * E:(t + 1) * E], xn2T[:, t * P:(t + 1) * P], gate_T[:, :], start=True, stop=True)
                elif kind == "wu":
                    pe.wait_ge(up_loaded[b % 2], 16 * (b // 2 + 1))
                    for c in range(IC):
                        ins = pe.transpose(W[:, c * P:(c + 1) * P], stage_up[:, b % 2, c, :], ident[:, :])
                elif kind == "wd":
                    pe.wait_ge(dn_loaded[b % 2], 16 * (b // 2 + 1))
                    for c in range(IC):
                        ins = pe.transpose(W[:, c * P:(c + 1) * P], stage_dn[:, b % 2, c * P:(c + 1) * P], ident[:, :])
                elif kind == "rt":
                    pe.wait_ge(chosen_ready, b + 1)
                    m = chosen[:, :, :].rearrange("p t e -> p (t e)")
                    pe.matmul(W[:, 0:HT * E], before[:, :], m, start=True, stop=True)
                    ins = pe.matmul(W[:, HT * E:2 * HT * E], ones[:, :], m, start=True, stop=True)
                ins.then_inc(step_done, 1)

            def scores(J):
                b, j = divmod(J, BT)
                if j == 0:
                    pe.wait_ge(act_drained, act_at[("kT", b, 1)])
                    pe.wait_ge(dve_drained, dve_at[("kT", b, 1)])
                if J >= 2:
                    pe.wait_ge(probs_ready, J - 1)
                keys = slice(j * P, (j + 1) * P)
                for g in range(QG):
                    cols = slice(g * 512, (g + 1) * 512)
                    ins = split3(psS[:, J % 2, cols], (kT_hi[:, b % 2, keys], kT_lo[:, b % 2, keys]),
                                 (qT_hi[:, b % 2, cols], qT_lo[:, b % 2, cols]))
                ins.then_inc(scores_done, 1)

            def pv(J):
                b, j = divmod(J, BT)
                pe.wait_ge(probs_ready, J + 1)
                if j == 0 and b > 0:
                    pe.wait_ge(oT_ready, b)
                for g in range(QG):
                    cols = slice(g * 512, (g + 1) * 512)
                    ins = pe.matmul(psO[:, cols], V[:, b % 2, j, :], probs[:, J % 2, cols], start=(j == 0), stop=(j == BT - 1))
                ins.then_inc(pv_done, 1)

            for what, J, s in plan:
                if what == "scores":
                    scores(J)
                elif what == "pv":
                    pv(J)
                else:
                    pe_step(s)

            def turn_x(par, xin_wait):
                pe.wait_ge(xin_loaded[par], xin_wait)
                pe.transpose(psX[:, par, 0:P], xin[:, par, :], ident[:, :]).then_inc(xT_done, 1)

            def up(par, t1, off):
                pe.wait_ge(xlo_ready, t1)
                dst = psU[:, par, :]
                pe.matmul(dst, xT_hi[:, par, :], wup_hi[:, bass.ds(off, I)], start=True, stop=False)
                pe.matmul(dst, xT_hi[:, par, :], wup_lo[:, bass.ds(off, I)], start=False, stop=False)
                pe.matmul(dst, xT_lo[:, par, :], wup_hi[:, bass.ds(off, I)], start=False, stop=True).then_inc(up_done, 1)

            def turn_h(par, t1):
                pe.wait_ge(hid_ready, t1)
                for c in range(IC):
                    ins = pe.transpose(psH[:, par, c * P:(c + 1) * P], hid[:, par, c * P:(c + 1) * P], ident[:, :])
                ins.then_inc(hT_done, 1)

            def down(par, t1, off):
                pe.wait_ge(hlo_ready, t1)
                for c in range(IC):
                    w = wdn[:, bass.ds(off * 2 + c * 2 * D, 2 * D)]
                    pe.matmul(psY[:, par, 0:2 * D], hT_hi[:, par, c * P:(c + 1) * P], w, start=(c == 0), stop=False)
                    ins = pe.matmul(psY[:, par, 0:2 * D], hT_lo[:, par, c * P:(c + 1) * P], w, start=False, stop=(c == IC - 1))
                ins.then_inc(down_done, 1)

            for h in range(HALVES):
                t0 = h * FT

                def offsets(i, n):
                    packed = pe.value_load(experts[0:1, h, bass.ds(i, 1)], min_val=0, max_val=16 ** 4 - 1)
                    return [pe.snap(((packed >> (4 * u)) & (E - 1)) * I) for u in range(n)]

                pe.wait_ge(routed, h + 1)
                if h == 0:
                    pe.wait_ge(act_drained, act_at[steps[-1]])
                    pe.wait_ge(dve_drained, dve_at[steps[-1]])
                    pe.wait_ge(oT_ready, B)
                    pe.wait_ge(probs_ready, NJ)

                def fill(i):
                    return 16 * ((t0 + i) // 2 + 1)

                offs = offsets(0, 2)
                turn_x(t0 % 2, fill(0))
                turn_x((t0 + 1) % 2, fill(1))
                up(t0 % 2, t0 + 1, offs[0])
                turn_x(t0 % 2, fill(2))
                up((t0 + 1) % 2, t0 + 2, offs[1])
                turn_x((t0 + 1) % 2, fill(3))
                turn_h(t0 % 2, t0 + 1)
                with pe.Fori(0, LOOPS) as k:
                    offs = offsets(k * 2, 4)
                    for u in range(2):
                        up((t0 + u) % 2, k * 2 + (t0 + u + 3), offs[u + 2])
                        turn_x((t0 + u) % 2, k * 16 + fill(u + 4))
                        down((t0 + u) % 2, k * 2 + (t0 + u + 1), offs[u])
                        turn_h((t0 + u + 1) % 2, k * 2 + (t0 + u + 2))
                last = 2 * LOOPS
                offs = offsets(last, 4) + (offsets(FT - 1, 1) if FT - last > 4 else [])
                for i in range(2 + last, FT + 2):
                    if i < FT:
                        up((t0 + i) % 2, t0 + i + 1, offs[i - last])
                    if i + 2 < FT:
                        turn_x((t0 + i) % 2, fill(i + 2))
                    down((t0 + i - 2) % 2, t0 + i - 1, offs[i - 2 - last])
                    if i - 1 < FT:
                        turn_h((t0 + i - 1) % 2, t0 + i)

        @block.vector
        def _(dve):
            own = Count(s_dve)

            def stats(dst_mv, src, base_t):
                for t in range(BT):
                    ins = dve.bn_stats(bst[:, t, :], src[:, base_t + t, :])
                own.settle(dve, ins)
                for t in range(BT):
                    ins = dve.bn_aggr(dst_mv[:, t, :], bst[:, t, :])
                return ins

            def stats_x(b):
                dve.wait_ge(x_loaded[b], 16)
                stats(mv_x, X, b * BT).then_inc(x_stats, 1)

            def normalise(dst, dst_t, src_t, mv, r):
                for t in range(BT):
                    ins = dve.tensor_scalar(dst[:, dst_t + t, :], X[:, src_t + t, :], mv[:, t, 0:1], r[:, t:t + 1],
                                            ALU.subtract, ALU.mult)
                return ins

            def norm_x(b):
                dve.wait_ge(rx_ready, b + 1)
                if b > 0:
                    dve.wait_ge(step_done, number[("xT", b - 1, 1)] + 1)
                normalise(xn, 0, b * BT, mv_x, r_x).then_inc(xn_ready, 1)

            def scale_k(b):
                dve.wait_ge(rk_ready, b + 1)
                for t in range(BT):
                    ins = dve.tensor_scalar(QK[:, t, 1, :], QK[:, t, 1, :], r_qk[:, 1, t:t + 1], None, ALU.mult)
                ins.then_inc(ks_ready, 1)

            def norm_n(b):
                dve.wait_ge(rn_ready, b + 1)
                normalise(XN2, b * BT, b * BT, mv_n, r_n).then_inc(xn2_ready, 1)

            def centre(dst, src, i, width=P):
                own.settle(dve, dve.tensor_reduce(wsum[:, i:i + 1], src, AX.X, ALU.add))
                own.settle(dve, dve.tensor_scalar(wsum[:, i:i + 1], wsum[:, i:i + 1], -1.0 / P, None, ALU.mult))
                ins = dve.tensor_scalar(dst, src, wsum[:, i:i + 1], None, ALU.add)
                return ins

            def dve_step(s):
                kind, b, g = s
                W = bank(s)
                if "V" not in READERS[kind]:
                    return
                dve.wait_ge(step_done, number[s] + 1)
                if "A" in READERS[kind]:
                    dve.wait_ge(act_drained, act_at[s])
                cols = slice(g * 512, (g + 1) * 512)
                if kind == "wa":
                    dve.wait_ge(row_loaded, 16 * 6)
                    own.settle(dve, centre(w_qkv[:, 0:P], W[:, 0:P], 0))
                    own.settle(dve, centre(w_qkv[:, P:2 * P], W[:, P:2 * P], 1))
                    own.settle(dve, dve.tensor_copy(w_qkv[:, 2 * P:3 * P], W[:, 2 * P:3 * P]))
                    ins = dve.tensor_tensor(scrap[:, :], W[:, 3 * P:4 * P], b_row[:, 4, :], ALU.mult)
                    ins.then_inc(dve_drained, 1)
                    dve.wait_ge(dve_drained, dve_at[s])
                    own.settle(dve, centre(w_o[:, :], scrap[:, :], 2))
                    own.settle(dve, centre(b_row[:, 0, :], b_row[:, 0, :], 3))
                    own.settle(dve, dve.tensor_tensor(b_row[:, 3, :], b_row[:, 3, :], b_row[:, 4, :], ALU.mult))
                    own.settle(dve, centre(b_row[:, 3, :], b_row[:, 3, :], 4))
                    own.settle(dve, centre(b_row[:, 1, :], b_row[:, 1, :], 5))
                    dve.engine_nop().then_inc(weights_ready, 1)
                    return
                if kind == "gt":
                    dve.tensor_copy(gate_T[:, :], W[:, 0:E]).then_inc(dve_drained, 1)
                elif kind == "qkv":
                    if g == 0 and b > 0:
                        dve.wait_ge(step_done, number[("kT", b - 1, 1)] + 1)
                        dve.wait_ge(rk_ready, b)
                        if b >= 2:
                            dve.wait_ge(pv_done, BT * (b - 1))
                    dve.tensor_tensor(QK[:, g, :, :], W[:, 0:2 * P].rearrange("p (a d) -> p a d", a=2), b_row[:, 0:2, :], ALU.add)
                    dve.tensor_tensor(V[:, b % 2, g, :], W[:, 2 * P:3 * P], b_row[:, 2, :], ALU.add).then_inc(dve_drained, 1)
                    dve.wait_ge(dve_drained, dve_at[s])
                    for a in range(2):
                        own.settle(dve, dve.tensor_tensor_reduce(out=scrap[:, :], in0=QK[:, g, a, :], in1=QK[:, g, a, :], scale=1.0, scalar=0.0,
                                                                 op0=ALU.mult, op1=ALU.add, accum_out=ss_qk[:, a, g:g + 1]))
                    if g == BT - 1:
                        dve.engine_nop().then_inc(qk_stats, 1)
                elif kind == "qT":
                    dve.tensor_tensor(qT_lo[:, b % 2, cols], W, qT_hi[:, b % 2, cols].bitcast(F32), ALU.subtract
                                      ).then_inc(dve_drained, 1)
                elif kind == "kT":
                    dve.tensor_tensor(kT_lo[:, b % 2, cols], W, kT_hi[:, b % 2, cols].bitcast(F32), ALU.subtract
                                      ).then_inc(dve_drained, 1)
                elif kind == "wd":
                    dve.tensor_tensor(wdn_parts(b)[:, :, 1, :], W.rearrange("p (c h) -> p c h", h=D), wdn_parts(b)[:, :, 0, :].bitcast(F32),
                                      ALU.subtract).then_inc(dve_drained, 1)
                elif kind == "wu":
                    e = slice(b * I, (b + 1) * I)
                    dve.tensor_tensor(wup_lo[:, e], W, wup_hi[:, e].bitcast(F32), ALU.subtract).then_inc(dve_drained, 1)
                elif kind == "pj":
                    bias = b_row[:, 3:4, :].to_broadcast([P, GT, D])
                    ins = dve.tensor_tensor(proj[:, g * GT:(g + 1) * GT, :], W.rearrange("p (t d) -> p t d", d=D), bias, ALU.add)
                    ins.then_inc(dve_drained, 1)
                    dve.wait_ge(dve_drained, dve_at[s])
                    for t in range(g * GT, (g + 1) * GT):
                        own.settle(dve, dve.tensor_tensor_reduce(out=scrap[:, :], in0=proj[:, t, :], in1=proj[:, t, :], scale=1.0, scalar=0.0,
                                                       op0=ALU.mult, op1=ALU.add, accum_out=ss_p[:, t:t + 1]))
                    if g == QG - 1:
                        dve.engine_nop().then_inc(p_stats, 1)
                elif kind == "lg":
                    bias = eb_row[:, :].unsqueeze(1).to_broadcast([P, BT, E])
                    ins = dve.tensor_tensor(L[:, b * BT:(b + 1) * BT, :], W[:, 0:BT * E].rearrange("p (t e) -> p t e", e=E), bias, ALU.add)
                    ins.then_inc(dve_drained, 1)
                    dve.wait_ge(dve_drained, dve_at[s])
                elif kind == "rt":
                    route_slots(b, W)
                    route_gates(b)

            def residual(b):
                dve.wait_ge(rp_ready, b + 1)
                for t in range(BT):
                    T = b * BT + t
                    ins = dve.scalar_tensor_tensor(out=X[:, T, :], in0=proj[:, t, :], scalar=r_p[:, t:t + 1], in1=X[:, T, :],
                                                   op0=ALU.mult, op1=ALU.add)
                own.settle(dve, ins)
                stats(mv_n, X, b * BT).then_inc(n_stats, 1)

            def over_e(v):
                return v.unsqueeze(2).to_broadcast([P, HT, E])

            def over_t(v):
                return v.unsqueeze(1).to_broadcast([P, HT, E])

            def pick(src, best, one_hot):
                own.settle(dve, dve.tensor_reduce(best, src, AX.X, ALU.max))
                own.settle(dve, dve.tensor_tensor(rb[:, :, :], src, over_e(best), ALU.is_equal))
                own.settle(dve, dve.tensor_tensor(rb[:, :, :], rb[:, :, :], over_t(desc[:, :]), ALU.mult))
                own.settle(dve, dve.tensor_reduce(kk[:, :], rb[:, :, :], AX.X, ALU.max))
                own.settle(dve, dve.tensor_tensor(one_hot, over_e(kk[:, :]), over_t(desc[:, :]), ALU.is_equal))

            def route_choose(h):
                Lh = L[:, h * HT:(h + 1) * HT, :]
                if h == 0:
                    dve.wait_ge(consts, 5)
                pick(Lh, m1[:, :], oh[0][:, :, :])
                own.settle(dve, dve.scalar_tensor_tensor(out=ra[:, :, :], in0=oh[0][:, :, :], scalar=-3.0e38, in1=Lh, op0=ALU.mult, op1=ALU.add))
                pick(ra[:, :, :], m2[:, :], oh[1][:, :, :])
                own.settle(dve, dve.tensor_tensor(ED[:, :, 0:E], Lh, over_e(m1[:, :]), ALU.subtract))
                own.settle(dve, dve.tensor_tensor(ED[:, :, E:E + 1], m2[:, :].unsqueeze(2), m1[:, :].unsqueeze(2), ALU.subtract))
                dve.engine_nop().then_inc(exp_in, 1)
                own.settle(dve, dve.tensor_tensor(chosen[:, :, :], oh[0][:, :, :], oh[1][:, :, :], ALU.add))
                dve.engine_nop().then_inc(chosen_ready, 1)

            def route_gates(h):
                dve.wait_ge(exp_out, h + 1)
                own.settle(dve, dve.tensor_reduce(zs[:, :], ED[:, :, 0:E], AX.X, ALU.add))
                own.settle(dve, dve.tensor_scalar(zs[:, :], zs[:, :], GATE_EPS, 1.0, ALU.mult, ALU.add))
                own.settle(dve, dve.tensor_tensor(zs[:, :], zs[:, :], ED[:, :, E], ALU.add))
                own.settle(dve, dve.reciprocal(gates[:, h, 0, :], zs[:, :]))
                own.settle(dve, dve.tensor_tensor(gates[:, h, 1, :], gates[:, h, 0, :], ED[:, :, E], ALU.mult))

            def route_slots(h, W):
                n = HT * E
                own.settle(dve, dve.tensor_copy(ra[:, :, :], W[:, 0:n].rearrange("p (t e) -> p t e", e=E)))
                ins = dve.tensor_copy(tot[:, :, :], W[:, n:2 * n].rearrange("p (t e) -> p e t", e=E))
                ins.then_inc(dve_drained, 1)
                dve.wait_ge(dve_drained, dve_at[("rt", h, 0)])
                flat = [v[:, :, :].rearrange("p e t -> p (e t)") for v in (incl, tot)]
                own.settle(dve, dve.tensor_tensor_scan(flat[0], seg[:, :], flat[1], 0.0, ALU.mult, ALU.add))
                count = incl[:, :, HT - 1:HT].to_broadcast([P, E, HT])
                own.settle(dve, dve.tensor_tensor(gtt[:, :, :], count, thr[:, :].unsqueeze(1).to_broadcast([P, E, HT]), ALU.is_gt))
                own.settle(dve, dve.tensor_reduce(ntile[:, :], gtt[:, :, :], AX.X, ALU.add))
                own.settle(dve, dve.tensor_tensor_scan(endt[:, :], ones[:, 0:E], ntile[:, :], 0.0, ALU.mult, ALU.add))
                own.settle(dve, dve.tensor_tensor(base[:, :], endt[:, :], ntile[:, :], ALU.subtract))
                own.settle(dve, dve.tensor_scalar(base[:, :], base[:, :], float(P), None, ALU.mult))
                own.settle(dve, dve.tensor_tensor(ext[:, :, :], endt[:, :].unsqueeze(1).to_broadcast([P, FT, E]),
                                                  tix[:, :].unsqueeze(2).to_broadcast([P, FT, E]), ALU.is_le))
                own.settle(dve, dve.tensor_reduce(exf[:, :], ext[:, :, :], AX.X, ALU.add))
                own.settle(dve, dve.tensor_scalar(exf[:, :], exf[:, :], float(E - 1), None, ALU.min))
                own.settle(dve, dve.tensor_copy(exp_packed[:, :], exf[:, :]))
                for u in range(1, 4):
                    own.settle(dve, dve.scalar_tensor_tensor(out=exp_packed[:, 0:FT - u], in0=exf[:, u:FT], scalar=float(16 ** u),
                                                             in1=exp_packed[:, 0:FT - u], op0=ALU.mult, op1=ALU.add))
                own.settle(dve, dve.tensor_copy(experts[:, h, :], exp_packed[:, :]))
                own.settle(dve, dve.tensor_tensor(incl[:, :, :], incl[:, :, :], tot[:, :, :], ALU.subtract))
                own.settle(dve, dve.tensor_tensor(ra[:, :, :], ra[:, :, :], incl[:, :, :].rearrange("p e t -> p t e"), ALU.add))
                own.settle(dve, dve.tensor_tensor(ra[:, :, :], ra[:, :, :], over_t(base[:, :]), ALU.add))
                for k in range(TOPK):
                    own.settle(dve, dve.tensor_tensor(rb[:, :, :], ra[:, :, :], oh[k][:, :, :], ALU.mult))
                    own.settle(dve, dve.tensor_reduce(slots_f[:, :], rb[:, :, :], AX.X, ALU.add))
                    own.settle(dve, dve.tensor_copy(slots[:, h, k, :], slots_f[:, :]))
                dve.engine_nop().then_inc(routed, 1)

            stats_x(0)
            norm_x(0)
            for what, J, s in plan:
                if s is not None and s[0] == "nT" and s[2] == 0:
                    norm_n(s[1])
                if s is not None and s[0] == "qT" and s[2] == 0:
                    scale_k(s[1])
                if what in ("step", "setup"):
                    dve_step(s)
                    if s[0] == "lg" and (s[1] + 1) % HB == 0:
                        route_choose(s[1] // HB)
                    if s == ("qkv", 0, 3):
                        stats_x(1)
                    if s == ("qkv", 0, BT - 1):
                        norm_x(1)
                    elif s[0] == "pj" and s[2] == QG - 1:
                        residual(s[1])
                if what == "scores" and J % BT == 3 and J // BT + 2 < B:
                    stats_x(J // BT + 2)
                if what == "scores" and J % BT == 7 and J // BT + 2 < B:
                    norm_x(J // BT + 2)

            def split_lo(par, wait):
                dve.wait_ge(xhi_ready, wait)
                dve.tensor_tensor(xT_lo[:, par, :], psX[:, par, 0:P], xT_hi[:, par, :].bitcast(F32), ALU.subtract
                                  ).then_inc(xlo_ready, 1)

            def split_h(par, wait):
                dve.wait_ge(hhi_ready, wait)
                dve.tensor_tensor(hT_lo[:, par, :], psH[:, par, :], hT_hi[:, par, :].bitcast(F32), ALU.subtract
                                  ).then_inc(hlo_ready, 1)

            def take_y(par, wait, stored_before):
                dve.wait_ge(down_done, wait)
                if stored_before is not None:
                    dve.wait_ge(y_stored[par], stored_before)
                dve.tensor_reduce(yo[:, par, :], psY[:, par, 0:2 * D].rearrange("p (a d) -> p d a", a=2), AX.X, ALU.add
                                  ).then_inc(yo_ready, 1)

            for h in range(HALVES):
                t0 = h * FT
                split_lo(t0 % 2, t0 + 1)
                split_lo((t0 + 1) % 2, t0 + 2)
                split_lo(t0 % 2, t0 + 3)
                split_lo((t0 + 1) % 2, t0 + 4)
                split_h(t0 % 2, t0 + 1)
                first = 2 if h == 0 else 0
                for i in range(2, 2 + first):
                    split_lo((t0 + i) % 2, t0 + i + 3)
                    take_y((t0 + i) % 2, t0 + i - 1, None)
                    split_h((t0 + i - 1) % 2, t0 + i)
                with dve.Fori(first // 2, LOOPS) as k:
                    for u in range(2):
                        split_lo((t0 + u) % 2, k * 2 + (t0 + u + 5))
                        take_y((t0 + u) % 2, k * 2 + (t0 + u + 1), k * 16 + 16 * ((t0 + u) // 2))
                        split_h((t0 + u + 1) % 2, k * 2 + (t0 + u + 2))
                for i in range(2 + 2 * LOOPS, FT + 2):
                    if i + 2 < FT:
                        split_lo((t0 + i) % 2, t0 + i + 3)
                    take_y((t0 + i) % 2, t0 + i - 1, 16 * ((t0 + i - 2) // 2))
                    if i - 1 < FT:
                        split_h((t0 + i - 1) % 2, t0 + i)

            def rsqrt(dst, src, n):
                own.settle(dve, dve.tensor_scalar(nv[:, 0:n], src, 1.0, LN_EPS, ALU.mult, ALU.add))
                own.up(dve.tensor_scalar(dst.bitcast(I32), nv[:, 0:n].bitcast(I32), -0.5, float(0x5f3759df), ALU.mult, ALU.add))
                own.settle(dve, dve.tensor_scalar(nh[:, 0:n], nv[:, 0:n], -0.5, None, ALU.mult))
                for _ in range(3):
                    own.settle(dve, dve.tensor_tensor(ntm[:, 0:n], dst, nh[:, 0:n], ALU.mult))
                    own.settle(dve, dve.tensor_tensor(ntm[:, 0:n], dst, ntm[:, 0:n], ALU.mult))
                    own.settle(dve, dve.scalar_tensor_tensor(out=dst, in0=ntm[:, 0:n], scalar=1.5, in1=dst, op0=ALU.add, op1=ALU.mult))

            for g in range(NT // BT):
                h = g * BT // HT
                T0 = g * BT
                fin = fz if g % 2 == 0 else xn
                dve.wait_ge(mixed0, g + 1)
                for t in range(BT):
                    ins = dve.scalar_tensor_tensor(out=fo[:, t, :], in0=G[g % 2][:, t, 1, :], scalar=gates[:, h, 1, T0 % HT + t:T0 % HT + t + 1],
                                                   in1=fo[:, t, :], op0=ALU.mult, op1=ALU.add)
                ins.then_inc(g_free, 1)
                dve.wait_ge(g_free, g + 1)
                own.settle(dve, stats(mv_n, fo, 0))
                rsqrt(r_n[:, :], mv_n[:, :, 1], BT)
                if g >= 2:
                    dve.wait_ge(stored[g - 2], 16)
                for t in range(BT):
                    ins = dve.tensor_scalar(fin[:, t, :], fo[:, t, :], mv_n[:, t, 0:1], r_n[:, t:t + 1], ALU.subtract, ALU.mult)
                ins.then_inc(f_in, 1)
                dve.wait_ge(f_in, 2 * g + 1)
                own.settle(dve, dve.tensor_tensor(fin[:, :, :], fin[:, :, :], XN2[:, T0:T0 + BT, :], ALU.add))
                own.settle(dve, stats(mv_n, fin, 0))
                rsqrt(r_n[:, :], mv_n[:, :, 1], BT)
                for t in range(BT):
                    ins = dve.tensor_scalar(fin[:, t, :], fin[:, t, :], mv_n[:, t, 0:1], r_n[:, t:t + 1], ALU.subtract, ALU.mult)
                ins.then_inc(f_in, 1)
                dve.wait_ge(f_in, 2 * g + 2)
                dve.tensor_tensor(fin[:, :, :], fin[:, :, :], X[:, T0:T0 + BT, :], ALU.add).then_inc(final_ready, 1)


_INS = ['L0_attn_x', 'L0_attn_Wq', 'L0_attn_bq', 'L0_attn_Wk', 'L0_attn_bk', 'L0_attn_Wv', 'L0_attn_bv', 'L0_attn_Wo',
        'L0_attn_bo', 'L0_attn_layerscale', 'L0_ffn_gate_w', 'L0_ffn_expert_bias', 'L0_ffn_w_up', 'L0_ffn_w_down']


def kernel(**inputs):
    import numpy as _np
    import concourse.bacc as _bacc
    from concourse import mybir as _mybir
    from concourse.bass_utils import run_bass_kernel_spmd as _run

    nc = _bacc.Bacc("TRN2", target_bir_lowering=False, num_devices=1)
    arrays, args = {}, []
    for name in _INS:
        a = _np.ascontiguousarray(inputs[name])
        arrays[f"in_{name}_dram"] = a
        args.append(nc.dram_tensor(f"in_{name}_dram", a.shape, _mybir.dt.from_np(a.dtype), kind="ExternalInput").ap())
    shape = inputs['L0_attn_x'].shape
    args.append(nc.dram_tensor("out_0_dram", shape, _mybir.dt.float32, kind="ExternalOutput").ap())
    build_program(nc, *args)
    r = _run(nc, [arrays], core_ids=[0])
    return r.results[0]["out_0_dram"]
```

```python
from contextlib import ExitStack

import numpy as np

import concourse.bass as bass
from concourse import mybir

F32 = mybir.dt.float32
F32R = mybir.dt.float32r
I32 = mybir.dt.int32
U32 = mybir.dt.uint32
ALU = mybir.AluOpType
ACT = mybir.ActivationFunctionType
AX = mybir.AxisListType

P = 128
LN_EPS = 1e-5
GATE_EPS = 1e-6


class Count:

    def __init__(self, sem):
        self.sem, self.n = sem, 0

    def up(self, ins):
        self.n += 1
        ins.then_inc(self.sem, 1)

    def settle(self, eng, ins):
        self.up(ins)
        eng.wait_ge(self.sem, self.n)


def build_program(nc, x, Wq, bq, Wk, bk, Wv, bv, Wo, bo, layerscale, gate_w, expert_bias, w_up, w_down, out):
    B, S, D = x.shape
    E, I, _ = w_up.shape
    assert D == P and S % 512 == 0 and I == 512
    BT = S // P
    NT = B * BT
    HALVES = 2
    HT = NT // HALVES
    HB = B // HALVES
    TOPK = 2
    FT = (HT * P * TOPK + E * (P - 1)) // P
    STEPS = FT + 3
    PEEL = (13, 25)
    UNROLL = 4
    LOOPS = [(FT - 6 - n) // UNROLL for n in PEEL]
    PACK = UNROLL + 3
    IC = I // P
    QG = S // 512
    GT = 512 // P
    LOG_S = float(np.log(np.float32(S)))
    K_SCALE = float(1.0 / np.sqrt(np.float32(D)))

    REC = D + 2
    xs = [nc.dram_tensor(f"sorted_x{h}", [FT * P, REC], F32, kind="Internal").ap() for h in range(HALVES)]
    zs_dram = [nc.dram_tensor(f"results{h}", [TOPK * (HT + FT) * P, D], F32, kind="Internal").ap() for h in range(HALVES)]

    x_t = x.rearrange("b (t p) d -> p (b t) d", p=P)
    out_t = out.rearrange("b (t p) d -> p (b t) d", p=P)

    with ExitStack() as ctx:
        def sb(name, shape, dt=F32):
            return ctx.enter_context(nc.sbuf_tensor(name, shape, dt))

        def sem(name):
            return ctx.enter_context(nc.semaphore(name))

        X = sb("X", [P, NT, D])
        rec = sb("rec", [P, NT, REC])
        XN2 = rec[:, :, 0:D]
        wup_hi = sb("wup_hi", [P, E * I], F32R)
        wup_lo = sb("wup_lo", [P, E * I], F32R)
        wdn = sb("wdn", [P, E * IC * 2 * D], F32R)
        stage_up = sb("stage_up", [P, 2, IC, P])
        stage_dn = sb("stage_dn", [P, 2, I])
        wnat = sb("wnat", [P, 4, P])
        w_qkv = sb("w_qkv", [P, 3 * P])
        w_o = sb("w_o", [P, P])
        bvT = sb("bvT", [P, P])
        b_row = sb("b_row", [P, 6, P])
        wsum = sb("wsum", [P, 8])
        gate_nat = sb("gate_nat", [E, P])
        gate_T = sb("gate_T", [P, E])
        eb_row = sb("eb_row", [P, E])
        ident = sb("ident", [P, P])
        ones = sb("ones", [P, P])
        before = sb("before", [P, P])
        no_token = sb("no_token", [P, 1, REC])
        neg_log_s = sb("neg_log_s", [P, 1])
        xn = sb("xn", [P, BT, D])
        xnT = sb("xnT", [P, S])
        kT_hi = sb("kT_hi", [P, 2, S], F32R)
        kT_lo = sb("kT_lo", [P, 2, S], F32R)
        qT_hi = sb("qT_hi", [P, 2, S], F32R)
        qT_lo = sb("qT_lo", [P, 2, S], F32R)
        QK = sb("QK", [P, BT, 2, P])
        V = sb("V", [P, 2, BT, D])
        probs = sb("probs", [P, 2, S])
        oT = sb("oT", [P, S])
        proj = sb("proj", [P, BT, D])
        xn2T = xnT
        scrap = sb("scrap", [P, GT, P])
        L = sb("L", [P, NT, E])
        bst = sb("bst", [P, BT, 6])
        mv = sb("mv", [P, BT, 2])
        ss_qk = sb("ss_qk", [P, 2, BT])
        ss_p = sb("ss_p", [P, BT])
        r_x = sb("r_x", [P, 2, BT])
        r_n = sb("r_n", [P, 2, BT])
        r_f = sb("r_f", [P, 8, BT // 2])
        r_qk = sb("r_qk", [P, 2, BT])
        r_p = sb("r_p", [P, BT])
        nv, ntm = (sb(n, [P, 2 * BT]) for n in ("newton_v", "newton_t"))
        desc = sb("desc", [P, E])
        seg = sb("seg", [P, E * HT])
        thr = sb("thr", [P, HT])
        tix = sb("tix", [P, FT])
        m1 = sb("m1", [P, HT])
        m2 = sb("m2", [P, HT])
        kk = sb("kk", [P, HT])
        oh = [sb(f"oh{k}", [P, HT, E]) for k in range(TOPK)]
        ra = sb("ra", [P, HT, E])
        rb = sb("rb", [P, HT, E])
        ED = sb("ED", [P, HT, E + 1])
        zs = sb("zs", [P, HT])
        chosen = sb("chosen", [P, HT, E])
        incl = sb("incl", [P, E, HT])
        tot = sb("tot", [P, E, HT])
        gtt = sb("gtt", [P, E, HT])
        ntile = sb("ntile", [P, E])
        endt = sb("endt", [P, E])
        base = sb("base", [P, E])
        ext = sb("ext", [P, FT, E])
        exf = sb("exf", [P, FT])
        exp_packed = sb("exp_packed", [P, FT])
        experts = sb("experts", [P, HALVES, FT], I32)
        gates = sb("gates", [P, HALVES, TOPK, HT])
        slots_f = sb("slots_f", [P, HT])
        slots = sb("slots", [P, HALVES, TOPK, HT], U32)
        tile_first = sb("tile_first", [P, HALVES, FT])
        goes_to = sb("goes_to", [P, FT, 2])
        rows_f = sb("rows_f", [P, FT])
        rows = sb("rows", [P, HALVES, FT], U32)
        xin = sb("xin", [P, 4, D])
        xT_hi = sb("xT_hi", [P, 2, P], F32R)
        xT_lo = sb("xT_lo", [P, 2, P], F32R)
        hid = probs[:, 0, :].rearrange("p (a i) -> p a i", a=2)
        hT_hi = kT_hi[:, 0, :].rearrange("p (a i) -> p a i", a=2)
        hT_lo = kT_lo[:, 0, :].rearrange("p (a i) -> p a i", a=2)
        yo = sb("yo", [P, 4, D])
        FP = BT // 2
        PARTS = NT // FP
        v_flat = V[:, :, :, :].rearrange("p a t d -> p (a t d)").rearrange("p (t k d) -> p t k d", k=TOPK, d=D)
        two = [buf[:, a * FP:(a + 1) * FP, :, :] for buf in (QK, v_flat) for a in range(2)]
        fo = [proj[:, a * FP:(a + 1) * FP, :] for a in range(2)]
        oT_flat = oT[:, :].rearrange("p (t d) -> p t d", d=D)
        fz = [buf[:, a * FP:(a + 1) * FP, :] for buf in (oT_flat, xn) for a in range(2)]
        r_of = [[r_f[:, 4 * n + 2 * a:4 * n + 2 * a + 2, :] for a in range(2)] for n in range(2)]

        psS = ctx.enter_context(nc.psum_tensor("psS", [P, 2, S], F32))
        psO = ctx.enter_context(nc.psum_tensor("psO", [P, S], F32))
        psW = ctx.enter_context(nc.psum_tensor("psW", [P, 2, 512], F32))
        psU = psS[:, 0, :].rearrange("p (a n) -> p a n", a=2)
        psH = psS[:, 1, :].rearrange("p (a n) -> p a n", a=2)
        psX = psO[:, 0:P]
        psY = psO[:, 512:512 + 2 * D]

        x_loaded = [sem(f"x_loaded{b}") for b in range(B)]
        w_loaded = sem("w_loaded")
        row_loaded = sem("row_loaded")
        up_loaded = [sem(f"up_loaded{i}") for i in range(2)]
        dn_loaded = [sem(f"dn_loaded{i}") for i in range(2)]
        cleared = sem("cleared")
        consts = sem("consts")
        weights_ready = sem("weights_ready")
        step_done = sem("step_done")
        act_drained = sem("act_drained")
        dve_drained = sem("dve_drained")
        scores_done = sem("scores_done")
        probs_ready = sem("probs_ready")
        pv_done = sem("pv_done")
        oT_ready = sem("oT_ready")
        x_std = sem("x_std")
        qk_std = sem("qk_std")
        n_std = sem("n_std")
        xn_ready = sem("xn_ready")
        qs_ready = sem("qs_ready")
        ks_ready = sem("ks_ready")
        xn2_ready = sem("xn2_ready")
        exp_in = sem("exp_in")
        exp_out = sem("exp_out")
        chosen_ready = sem("chosen_ready")
        routed = sem("routed")
        scattered = [sem(f"scattered{h}") for h in range(HALVES)]
        xin_loaded = [sem(f"xin_loaded{i}") for i in range(4)]
        xT_done = sem("xT_done")
        xhi_ready = sem("xhi_ready")
        xlo_ready = sem("xlo_ready")
        up_done = sem("up_done")
        hid_ready = sem("hid_ready")
        hT_done = sem("hT_done")
        hhi_ready = sem("hhi_ready")
        hlo_ready = sem("hlo_ready")
        down_done = sem("down_done")
        yo_ready = sem("yo_ready")
        goes_loaded = sem("goes_loaded")
        rows_found = sem("rows_found")
        y_scattered = [sem(f"y_scattered{i}") for i in range(4)]
        z_loaded = [sem(f"z_loaded{q}") for q in range(PARTS)]
        mixed0 = sem("mixed0")
        mixed = sem("mixed")
        f_std = sem("f_std")
        f_norm = sem("f_norm")
        f_added = sem("f_added")
        f_std2 = sem("f_std2")
        f_norm2 = sem("f_norm2")
        final_ready = sem("final_ready")
        stored = [sem(f"stored{q}") for q in range(PARTS)]
        s_dve, s_pool = sem("dve_own"), sem("pool_own")

        def front(b):
            return {0: [("xT", b, 0), ("xT", b, 1)], 1: [("qkv", b, t) for t in range(0, 3)],
                    2: [("qkv", b, t) for t in range(3, 6)], 3: [("qkv", b, t) for t in range(6, BT)],
                    5: [("qT", b, 0)], 6: [("qT", b, 1), ("kT", b, 0)], 7: [("kT", b, 1)]}

        def back(b):
            return {1: [("pj", b, 0)], 2: [("pj", b, 1)], 6: [("nT", b, 0)], 7: [("nT", b, 1), ("lg", b, 0)]}

        def weights_of(J):
            b, j = divmod(J, BT)
            n = {0: 0, 4: 1, 5: 2, 7: 3}.get(j)
            return [] if n is None else [("wu" if n % 2 == 0 else "wd", 2 * b + n // 2, 0)]

        def own_work(b):
            return {3: [("std_qk", b + 1), ("residual", b - 1)], 4: [("scale_q", b + 1), ("stats_x", b + 2)], 5: [("scale_k", b + 1), ("norm_n", b - 1)],
                    7: [("norm_x", b + 2)]}

        OWN_OF = {"std_qk": range(B), "scale_q": range(B), "scale_k": range(B), "stats_x": range(B), "norm_x": range(B),
                  "residual": range(B), "norm_n": range(B)}

        plan = [("setup", -1, s) for s in (("wa", 0, 0), ("gt", 0, 0), ("wv", 0, 0))]
        plan = [("own", ("stats_x", 0), None), ("own", ("norm_x", 0), None)] + plan
        for s in range(8):
            plan += [("step", -1, st) for st in front(0).get(s, [])]
            if s == 2:
                plan += [("own", ("stats_x", 1), None)]
            if s == 3:
                plan += [("own", (w, 0), None) for w in ("std_qk", "scale_q", "scale_k")]
        plan += [("own", ("norm_x", 1), None)]
        NJ = B * BT
        for J in range(NJ):
            b, j = divmod(J, BT)
            plan.append(("scores", J, None))
            if b > 0:
                plan += [("step", J, st) for st in back(b - 1).get(j, [])]
            if b + 1 < B:
                plan += [("step", J, st) for st in front(b + 1).get(j, [])]
            plan += [("step", J, st) for st in weights_of(J)]
            plan += [("own", w, None) for w in own_work(b).get(j, []) if w[1] in OWN_OF[w[0]]]
            if b > HB and (b - 1) % HB == 0 and j == 1:
                plan.append(("step", J, ("rt", (b - 1) // HB - 1, 0)))
            if J > 0:
                plan.append(("pv", J - 1, None))
        plan.append(("pv", NJ - 1, None))
        plan += [("step", NJ, s) for s in (("pj", B - 1, 0), ("pj", B - 1, 1))]
        plan += [("own", w, None) for w in (("residual", B - 1), ("norm_n", B - 1))]
        plan += [("step", NJ, s) for s in (("nT", B - 1, 0), ("nT", B - 1, 1), ("lg", B - 1, 0))]
        ROUTE_AT = 3
        for i in range(PEEL[0]):
            plan.append(("expert", i, None))
            if i == ROUTE_AT:
                plan.append(("step", NJ, ("rt", HALVES - 1, 0)))

        final_beside = {}
        for q in range(PARTS // 2):
            for n, kind in {0: "mix", 2: "norm", 3: "stat2", 5: "norm2"}.items():
                final_beside.setdefault(1 + 6 * q + n, []).append((kind, q))
        final_after = []
        for c in range(PARTS // 2, PARTS + 2):
            final_after += [(kind, q) for kind, q in (("mix", c), ("norm", c - 1), ("stat2", c - 1), ("norm2", c - 2)) if PARTS // 2 <= q < PARTS]

        READERS = {"wa": "V", "gt": "V", "wv": "V", "xT": "A", "qkv": "V", "qT": "AV", "kT": "AV", "pj": "V",
                   "nT": "A", "lg": "V", "wu": "AV", "wd": "AV", "rt": "V"}
        steps = [s for _, _, s in plan if s is not None]
        number = {s: n for n, s in enumerate(steps)}
        act_at, dve_at, na, nd = {}, {}, 0, 0
        for s in steps:
            na += "A" in READERS[s[0]]
            nd += "V" in READERS[s[0]]
            act_at[s], dve_at[s] = na, nd

        def bank(s):
            return psW[:, number[s] % 2, :]

        def wdn_parts(e):
            return wdn[:, 2 * e * I:2 * (e + 1) * I].rearrange("p (c a h) -> p c a h", a=2, h=D)

        block = ctx.enter_context(nc.Block())

        @block.sync
        def _(sp):
            sp.dma_start(X[:, 0:BT, :], x_t[:, 0:BT, :]).then_inc(x_loaded[0], 16)
            for i, w in enumerate((Wq, Wk, Wv, Wo)):
                sp.dma_start(wnat[:, i, :], w).then_inc(w_loaded, 16)
            for i, r in enumerate((bq, bk, bv, bo, layerscale)):
                sp.dma_start(b_row[:, i, :], r.rearrange("(a d) -> a d", a=1).to_broadcast([P, D])).then_inc(row_loaded, 16)
            sp.dma_start(eb_row[:, :], expert_bias.rearrange("(a d) -> a d", a=1).to_broadcast([P, E])).then_inc(row_loaded, 16)
            sp.dma_start(gate_nat[:, :], gate_w).then_inc(w_loaded, 16)
            for b in range(1, B):
                sp.dma_start(X[:, b * BT:(b + 1) * BT, :], x_t[:, b * BT:(b + 1) * BT, :]).then_inc(x_loaded[b], 16)
            sp.wait_ge(consts, 4)
            for h in range(HALVES):
                sp.dma_start(xs[h].rearrange("(r p) d -> p r d", p=P), no_token[:, :, :].to_broadcast([P, FT, REC])).then_inc(cleared, 16)
            for e in range(E):
                if e >= 2:
                    sp.wait_ge(step_done, number[("wd", e - 2, 0)] + 1)
                sp.dma_start(stage_up[:, e % 2, :, :], w_up[e].rearrange("(c p) h -> p c h", p=P)).then_inc(up_loaded[e % 2], 16)
                sp.dma_start(stage_dn[:, e % 2, :], w_down[e]).then_inc(dn_loaded[e % 2], 16)

            def load_results(q):
                h = q * FP // HT
                if q * FP % HT == 0:
                    for r in range(4):
                        sp.wait_ge(y_scattered[r], 16 * len([t for t in range((h + 1) * FT) if t % 4 == r]))
                if q >= 4:
                    sp.wait_ge(mixed, q - 3)
                t = q * FP % HT
                src = zs_dram[h][TOPK * t * P:TOPK * (t + FP) * P, :].rearrange("(t p k) d -> p t k d", p=P, k=TOPK)
                sp.dma_start(two[q % 4], src).then_inc(z_loaded[q], 16)

            def store_final(q):
                sp.wait_ge(final_ready, q + 1)
                sp.dma_start(out_t[:, q * FP:(q + 1) * FP, :], fz[q % 4]).then_inc(stored[q], 16)

            for h in range(HALVES):
                t0 = h * FT
                sp.wait_ge(scattered[h], 16 * HT * TOPK)

                def load(i, k=0):
                    t = t0 + i
                    if i >= UNROLL or h > 0:
                        sp.wait_ge(xT_done, UNROLL * k + t - UNROLL + 1)
                    sp.dma_start(xin[:, t % 4, :], xs[h][bass.ds(UNROLL * P * k + i * P, P), 0:D]).then_inc(xin_loaded[t % 4], 16)

                def step(i, k=0):
                    if i + 6 < FT:
                        load(i + 6, k)

                for i in range(6):
                    load(i)
                    if i == 3:
                        if h > 0:
                            sp.wait_ge(rows_found, h)
                        sp.dma_start(goes_to[:, :, :], xs[h].rearrange("(r p) d -> p r d", p=P)[:, :, D:D + 2]).then_inc(goes_loaded, 16)
                for i in range(PEEL[h]):
                    step(i)
                    if h == HALVES - 1:
                        if i == 0:
                            for q in range(PARTS // 2):
                                load_results(q)
                        for kind, q in final_beside.get(i - 2, []):
                            if kind == "norm2" and q < PARTS // 2 - 1:
                                store_final(q)
                with sp.Fori(0, LOOPS[h]) as k:
                    for u in range(UNROLL):
                        step(PEEL[h] + u, k)
                for i in range(PEEL[h] + UNROLL * LOOPS[h], STEPS):
                    step(i)
            store_final(PARTS // 2 - 1)
            for q in range(PARTS // 2, PARTS):
                load_results(q)
            for q in range(PARTS // 2, PARTS):
                store_final(q)
            for q in range(PARTS):
                sp.wait_ge(stored[q], 16)

        @block.gpsimd
        def _(pool):
            own = Count(s_pool)
            own.settle(pool, pool.memset(ident[:, :], 0.0))
            pool.affine_select(out=ident[:, :], in_=ident[:, :], compare_op=ALU.not_equal, fill=1.0, base=0,
                               pattern=[[-1, P]], channel_multiplier=1).then_inc(consts, 1)
            own.settle(pool, pool.memset(no_token[:, :, :], 0.0))
            pool.iota(no_token[:, 0, D:D + 1], pattern=[[0, 1]], base=TOPK * HT * P, channel_multiplier=TOPK,
                      allow_small_or_imprecise_dtypes=True).then_inc(consts, 1)
            own.settle(pool, pool.memset(ones[:, :], 1.0))
            pool.affine_select(out=before[:, :], in_=ones[:, :], compare_op=ALU.is_gt, fill=0.0, base=0,
                               pattern=[[1, P]], channel_multiplier=-1).then_inc(consts, 1)
            pool.memset(neg_log_s[:, :], -LOG_S).then_inc(consts, 1)
            for e in range(E):
                pool.memset(desc[:, e:e + 1], float(E - e))
            pool.memset(seg[:, :], 1.0)
            own.settle(pool, pool.iota(tix[:, :], pattern=[[1, FT]], base=0, channel_multiplier=0, allow_small_or_imprecise_dtypes=True))
            own.settle(pool, pool.tensor_scalar(thr[:, :], tix[:, 0:HT], float(P), None, ALU.mult))
            pool.memset(seg[:, :].rearrange("p (e t) -> p e t", t=HT)[:, :, 0:1], 0.0).then_inc(consts, 1)

            own.settle(pool, pool.iota(slots_f[:, :], pattern=[[TOPK * P, HT]], base=0, channel_multiplier=TOPK,
                                       allow_small_or_imprecise_dtypes=True))
            for h in range(HALVES):
                own.up(pool.tensor_copy(rec[:, h * HT:(h + 1) * HT, D:D + 1], slots_f[:, :].unsqueeze(2)))
            pool.wait_ge(own.sem, own.n)
            pool.engine_nop().then_inc(consts, 1)

            def scatter(h, t):
                for c in range(TOPK):
                    pool.indirect_dma_start(xs[h][:, :], bass.IndirectOffsetOnAxis(ap=slots[:, h, c, t:t + 1], axis=0),
                                            rec[:, h * HT + t, :], None).then_inc(scattered[h], 16)

            def scatter_y(h, i):
                t = h * FT + i
                pool.wait_ge(yo_ready, t + 1)
                pool.indirect_dma_start(zs_dram[h][:, :], bass.IndirectOffsetOnAxis(ap=rows[:, h, i:i + 1], axis=0),
                                        yo[:, t % 4, :], None).then_inc(y_scattered[t % 4], 16)

            pool.wait_ge(cleared, 16 * HALVES)
            pool.wait_ge(xn2_ready, HB)
            pool.wait_ge(routed, 1)
            for t in range(HT):
                scatter(0, t)
            pool.wait_ge(rows_found, 1)
            turn = FT - 2 * HT
            for i in range(turn):
                scatter_y(0, i)
            pool.wait_ge(xn2_ready, B)
            pool.wait_ge(routed, HALVES)
            for t in range(2):
                scatter(1, t)
            for i in range(turn, FT):
                scatter_y(0, i)
                if (i - turn) % 2 == 1 and (i - turn) // 2 + 2 < HT:
                    scatter(1, (i - turn) // 2 + 2)
            pool.wait_ge(rows_found, 2)

            def final_piece(kind, q):
                T0, fin = q * FP, fz[q % 4]
                if kind == "norm":
                    pool.wait_ge(f_norm, q + 1)
                    pool.tensor_tensor(fin, fin, XN2[:, T0:T0 + FP, :], ALU.add).then_inc(f_added, 1)
                elif kind == "norm2":
                    pool.wait_ge(f_norm2, q + 1)
                    pool.tensor_tensor(fin, fin, X[:, T0:T0 + FP, :], ALU.add).then_inc(final_ready, 1)

            for i in range(STEPS):
                if i - 3 >= 0:
                    scatter_y(1, i - 3)
                for piece in final_beside.get(i, []):
                    final_piece(*piece)
            for piece in final_after:
                final_piece(*piece)

        @block.scalar
        def _(act):
            def act_step(s):
                kind, b, g = s
                W = bank(s)
                if "A" not in READERS[kind]:
                    return
                act.wait_ge(step_done, number[s] + 1)
                cols = slice(g * 512, (g + 1) * 512)
                if kind == "xT":
                    act.activation(xnT[:, cols], W, ACT.Copy).then_inc(act_drained, 1)
                elif kind == "qT":
                    act.activation(qT_hi[:, b % 2, cols], W, ACT.Copy).then_inc(act_drained, 1)
                elif kind == "kT":
                    act.activation(kT_hi[:, b % 2, cols], W, ACT.Copy).then_inc(act_drained, 1)
                elif kind == "nT":
                    act.activation(xn2T[:, cols], W, ACT.Copy).then_inc(act_drained, 1)
                elif kind == "wu":
                    act.activation(wup_hi[:, b * I:(b + 1) * I], W, ACT.Copy).then_inc(act_drained, 1)
                elif kind == "wd":
                    act.activation(wdn_parts(b)[:, :, 0, :], W.rearrange("p (c h) -> p c h", h=D), ACT.Copy).then_inc(act_drained, 1)

            def route_exp(h):
                act.wait_ge(exp_in, h + 1)
                act.activation(ED[:, :, :], ED[:, :, :], ACT.Exp).then_inc(exp_out, 1)

            def own_work_of_act(name, b):
                if name == "norm_x":
                    act.wait_ge(x_std, b + 1)
                    if b > 0:
                        act.wait_ge(step_done, number[("xT", b - 1, 1)] + 1)
                    for t in range(BT):
                        ins = act.activation(xn[:, t, :], X[:, b * BT + t, :], ACT.Identity, bias=r_x[:, 1, t:t + 1], scale=r_x[:, 0, t:t + 1])
                    ins.then_inc(xn_ready, 1)
                elif name in ("scale_q", "scale_k"):
                    a = int(name == "scale_k")
                    if a == 0:
                        act.wait_ge(qk_std, b + 1)
                    for t in range(BT):
                        ins = act.activation(QK[:, t, a, :], QK[:, t, a, :], ACT.Copy, scale=r_qk[:, a, t:t + 1])
                    ins.then_inc((qs_ready, ks_ready)[a], 1)
                elif name == "norm_n":
                    act.wait_ge(n_std, b + 1)
                    for t in range(BT):
                        ins = act.activation(XN2[:, b * BT + t, :], X[:, b * BT + t, :], ACT.Identity, bias=r_n[:, 1, t:t + 1],
                                             scale=r_n[:, 0, t:t + 1])
                    ins.then_inc(xn2_ready, 1)

            def expert_step(h, i, k=0):
                t, k4 = h * FT + i, UNROLL * k
                if 0 <= i < FT:
                    act.wait_ge(up_done, k4 + t + 1)
                    act.activation(hid[:, t % 2, :], psU[:, t % 2, :], ACT.Gelu).then_inc(hid_ready, 1)
                if i + 2 < FT:
                    act.wait_ge(xT_done, k4 + t + 3)
                    act.activation(xT_hi[:, t % 2, :], psX, ACT.Copy).then_inc(xhi_ready, 1)
                if 0 <= i - 1 < FT:
                    act.wait_ge(hT_done, k4 + t)
                    act.activation(hT_hi[:, (t - 1) % 2, :], psH[:, (t - 1) % 2, :], ACT.Copy).then_inc(hhi_ready, 1)

            def first_tiles(h):
                for i in range(-2, 0):
                    expert_step(h, i)

            def final_piece(kind, q):
                h, T0 = q * FP // HT, q * FP % HT
                if kind == "mix":
                    act.wait_ge(z_loaded[q], 16)
                    if q >= 2:
                        act.wait_ge(f_norm, q - 1)
                    for t in range(FP):
                        ins = act.activation(fo[q % 2][:, t, :], two[q % 4][:, t, 0, :], ACT.Copy, scale=gates[:, h, 0, T0 + t:T0 + t + 1])
                    ins.then_inc(mixed0, 1)
                elif kind == "norm":
                    act.wait_ge(f_std, q + 1)
                    if q >= 4:
                        act.wait_ge(stored[q - 4], 16)
                    r = r_of[0][q % 2]
                    for t in range(FP):
                        ins = act.activation(fz[q % 4][:, t, :], fo[q % 2][:, t, :], ACT.Identity, bias=r[:, 1, t:t + 1], scale=r[:, 0, t:t + 1])
                    ins.then_inc(f_norm, 1)
                elif kind == "norm2":
                    act.wait_ge(f_std2, q + 1)
                    r = r_of[1][q % 2]
                    for t in range(FP):
                        ins = act.activation(fz[q % 4][:, t, :], fz[q % 4][:, t, :], ACT.Identity, bias=r[:, 1, t:t + 1], scale=r[:, 0, t:t + 1])
                    ins.then_inc(f_norm2, 1)

            for what, J, s in plan:
                if what == "own":
                    own_work_of_act(*J)
                elif what == "scores":
                    b, j = divmod(J, BT)
                    if J == 0:
                        act.wait_ge(consts, 4)
                    act.wait_ge(scores_done, J + 1)
                    if J >= 2:
                        act.wait_ge(pv_done, J - 1)
                    act.activation(probs[:, J % 2, :], psS[:, J % 2, :], ACT.Sigmoid, bias=neg_log_s[:, 0:1],
                                   scale=K_SCALE).then_inc(probs_ready, 1)
                elif what == "pv":
                    if J % BT == BT - 1:
                        act.wait_ge(pv_done, J + 1)
                        if J // BT > 0:
                            act.wait_ge(step_done, number[("pj", J // BT - 1, 1)] + 1)
                        act.activation(oT[:, :], psO[:, :], ACT.Copy).then_inc(oT_ready, 1)
                elif what == "expert":
                    if J == 0:
                        first_tiles(0)
                    expert_step(0, J)
                elif s[0] == "rt":
                    route_exp(s[1])
                else:
                    act_step(s)

            for h in range(HALVES):
                if h > 0:
                    first_tiles(h)
                    for i in range(PEEL[h]):
                        expert_step(h, i)
                        for piece in final_beside.get(i, []):
                            final_piece(*piece)
                with act.Fori(0, LOOPS[h]) as k:
                    for u in range(UNROLL):
                        expert_step(h, PEEL[h] + u, k)
                for i in range(PEEL[h] + UNROLL * LOOPS[h], STEPS):
                    expert_step(h, i)
            for piece in final_after:
                final_piece(*piece)

        @block.tensor
        def _(pe):
            pe.wait_ge(consts, 5)

            def split3(dst, lhs, rhs, start=True, stop=True):
                pe.matmul(dst, lhs[0], rhs[0], start=True, stop=False)
                pe.matmul(dst, lhs[0], rhs[1], start=False, stop=False)
                return pe.matmul(dst, lhs[1], rhs[0], start=False, stop=True)

            def pe_step(s):
                kind, b, g = s
                W = bank(s)
                if number[s] >= 2:
                    last = steps[number[s] - 2]
                    if "A" in READERS[last[0]]:
                        pe.wait_ge(act_drained, act_at[last])
                    if "V" in READERS[last[0]]:
                        pe.wait_ge(dve_drained, dve_at[last])
                cols = slice(g * 512, (g + 1) * 512)
                if kind == "wa":
                    pe.wait_ge(w_loaded, 16 * 5)
                    pe.wait_ge(row_loaded, 16 * 6)
                    for i in range(4):
                        ins = pe.transpose(W[:, i * P:(i + 1) * P], wnat[:, i, :], ident[:, :])
                elif kind == "gt":
                    pe.transpose(W[:, 0:E], gate_nat[:, :], ident[0:E, 0:E])
                    ins = pe.transpose(W[:, P:2 * P], b_row[:, 2, :], ident[:, :])
                elif kind == "wv":
                    pe.wait_ge(weights_ready, 1)
                    pe.matmul(W[:, 0:P], wnat[:, 2, :], w_o[:, :], start=True, stop=True)
                    ins = pe.matmul(W[:, P:2 * P], bvT[:, :], w_o[:, :], start=True, stop=True)
                elif kind == "xT":
                    pe.wait_ge(xn_ready, b + 1)
                    for t in range(GT):
                        ins = pe.transpose(W[:, t * P:(t + 1) * P], xn[:, g * GT + t, :], ident[:, :])
                elif kind == "qkv":
                    if g == 0:
                        pe.wait_ge(act_drained, act_at[("xT", b, 1)])
                        if b == 0:
                            pe.wait_ge(weights_ready, 2)
                    ins = pe.matmul(W[:, 0:3 * P], xnT[:, g * P:(g + 1) * P], w_qkv[:, :], start=True, stop=True)
                elif kind in ("qT", "kT"):
                    if kind == "qT":
                        pe.wait_ge(qs_ready, b + 1)
                    else:
                        pe.wait_ge(ks_ready, b + 1)
                    for t in range(GT):
                        ins = pe.transpose(W[:, t * P:(t + 1) * P], QK[:, g * GT + t, int(kind == "kT"), :], ident[:, :])
                elif kind == "pj":
                    pe.wait_ge(oT_ready, b + 1)
                    for t in range(GT):
                        tt = g * GT + t
                        ins = pe.transpose(W[:, t * P:(t + 1) * P], oT[:, tt * P:(tt + 1) * P], ident[:, :])
                elif kind == "nT":
                    pe.wait_ge(xn2_ready, b + 1)
                    for t in range(GT):
                        ins = pe.transpose(W[:, t * P:(t + 1) * P], XN2[:, b * BT + g * GT + t, :], ident[:, :])
                elif kind == "lg":
                    pe.wait_ge(act_drained, act_at[("nT", b, 1)])
                    for t in range(BT):
                        ins = pe.matmul(W[:, t * E:(t + 1) * E], xn2T[:, t * P:(t + 1) * P], gate_T[:, :], start=True, stop=True)
                elif kind == "wu":
                    pe.wait_ge(up_loaded[b % 2], 16 * (b // 2 + 1))
                    for c in range(IC):
                        ins = pe.transpose(W[:, c * P:(c + 1) * P], stage_up[:, b % 2, c, :], ident[:, :])
                elif kind == "wd":
                    pe.wait_ge(dn_loaded[b % 2], 16 * (b // 2 + 1))
                    for c in range(IC):
                        ins = pe.transpose(W[:, c * P:(c + 1) * P], stage_dn[:, b % 2, c * P:(c + 1) * P], ident[:, :])
                elif kind == "rt":
                    pe.wait_ge(chosen_ready, b + 1)
                    m = chosen[:, :, :].rearrange("p t e -> p (t e)")
                    pe.matmul(W[:, 0:HT * E], before[:, :], m, start=True, stop=True)
                    ins = pe.matmul(W[:, HT * E:2 * HT * E], ones[:, :], m, start=True, stop=True)
                ins.then_inc(step_done, 1)

            def scores(J):
                b, j = divmod(J, BT)
                if j == 0:
                    pe.wait_ge(act_drained, act_at[("kT", b, 1)])
                    pe.wait_ge(dve_drained, dve_at[("kT", b, 1)])
                if J >= 2:
                    pe.wait_ge(probs_ready, J - 1)
                keys = slice(j * P, (j + 1) * P)
                for g in range(QG):
                    cols = slice(g * 512, (g + 1) * 512)
                    ins = split3(psS[:, J % 2, cols], (kT_hi[:, b % 2, keys], kT_lo[:, b % 2, keys]),
                                 (qT_hi[:, b % 2, cols], qT_lo[:, b % 2, cols]))
                ins.then_inc(scores_done, 1)

            def pv(J):
                b, j = divmod(J, BT)
                pe.wait_ge(probs_ready, J + 1)
                if j == 0 and b > 0:
                    pe.wait_ge(oT_ready, b)
                for g in range(QG):
                    cols = slice(g * 512, (g + 1) * 512)
                    ins = pe.matmul(psO[:, cols], V[:, b % 2, j, :], probs[:, J % 2, cols], start=(j == 0), stop=(j == BT - 1))
                ins.then_inc(pv_done, 1)

            def turn_x(t, k, loads):
                pe.wait_ge(xin_loaded[t % 4], 16 * k + loads)
                if t > 0:
                    pe.wait_ge(xlo_ready, UNROLL * k + t)
                pe.transpose(psX, xin[:, t % 4, :], ident[:, :]).then_inc(xT_done, 1)

            def up(t, k, off):
                pe.wait_ge(xlo_ready, UNROLL * k + t + 1)
                dst, w = psU[:, t % 2, :], bass.ds(off, I)
                pe.matmul(dst, xT_hi[:, t % 2, :], wup_hi[:, w], start=True, stop=False)
                pe.matmul(dst, xT_hi[:, t % 2, :], wup_lo[:, w], start=False, stop=False)
                pe.matmul(dst, xT_lo[:, t % 2, :], wup_hi[:, w], start=False, stop=True).then_inc(up_done, 1)

            def turn_h(t, k):
                pe.wait_ge(hid_ready, UNROLL * k + t + 1)
                for c in range(IC):
                    ins = pe.transpose(psH[:, t % 2, c * P:(c + 1) * P], hid[:, t % 2, c * P:(c + 1) * P], ident[:, :])
                ins.then_inc(hT_done, 1)

            def down(t, k, off):
                pe.wait_ge(hlo_ready, UNROLL * k + t + 1)
                if t > 0:
                    pe.wait_ge(yo_ready, UNROLL * k + t)
                for c in range(IC):
                    w = wdn[:, bass.ds(off * 2 + c * 2 * D, 2 * D)]
                    pe.matmul(psY, hT_hi[:, t % 2, c * P:(c + 1) * P], w, start=(c == 0), stop=False)
                    ins = pe.matmul(psY, hT_lo[:, t % 2, c * P:(c + 1) * P], w, start=False, stop=(c == IC - 1))
                ins.then_inc(down_done, 1)

            def expert_step(h, i, k, offs):
                t = h * FT + i
                if 0 <= i < FT:
                    up(t, k, offs[1])
                if i + 2 < FT:
                    turn_x(t + 2, k, 16 * ((t + 2) // 4 + 1))
                if 0 <= i - 3:
                    down(t - 3, k, offs[0])
                if 0 <= i - 1 < FT:
                    turn_h(t - 1, k)

            def offsets(h, i, n):
                packed = pe.value_load(experts[0:1, h, bass.ds(i, 1)], min_val=0, max_val=E ** PACK - 1)
                return [pe.snap(((packed >> (3 * u)) & (E - 1)) * I) for u in range(n)]

            def peeled(h, i, known={}):
                first = i - i % UNROLL
                at = min(max(first - 3, 0), FT - 1)
                if known.get("at") != (h, at):
                    known["at"], known["offs"] = (h, at), offsets(h, at, min(PACK, FT - at))
                o = known["offs"]
                expert_step(h, i, 0, (o[i - 3 - at] if i >= 3 else None, o[i - at] if 0 <= i < FT else None))

            def first_tiles(h):
                pe.wait_ge(routed, h + 1)
                if h == 0:
                    pe.wait_ge(oT_ready, B)
                    pe.wait_ge(probs_ready, NJ)
                    pe.wait_ge(act_drained, act_at[("wd", E - 1, 0)])
                    pe.wait_ge(dve_drained, dve_at[("wd", E - 1, 0)])
                for i in range(-2, 0):
                    expert_step(h, i, 0, None)

            for what, J, s in plan:
                if what == "scores":
                    scores(J)
                elif what == "pv":
                    pv(J)
                elif what == "expert":
                    if J == 0:
                        first_tiles(0)
                    peeled(0, J)
                elif what != "own":
                    pe_step(s)

            for h in range(HALVES):
                if h > 0:
                    first_tiles(h)
                    for i in range(PEEL[h]):
                        peeled(h, i)
                n = PEEL[h]
                with pe.Fori(0, LOOPS[h]) as k:
                    offs = offsets(h, k * UNROLL + (n - 3), PACK)
                    for u in range(UNROLL):
                        expert_step(h, n + u, k, (offs[u], offs[u + 3]))
                for i in range(n + UNROLL * LOOPS[h], STEPS):
                    peeled(h, i)

        @block.vector
        def _(dve):
            own = Count(s_dve)

            def rsqrt(dst, src, scale, n):
                v, t = nv[:, 0:n], ntm[:, 0:n]
                own.settle(dve, dve.tensor_scalar(v, src, scale, LN_EPS, ALU.mult, ALU.add))
                own.settle(dve, dve.tensor_scalar(dst.bitcast(I32), v.bitcast(I32), -0.5, float(0x5f3759df), ALU.mult, ALU.add))
                own.settle(dve, dve.tensor_scalar(v, v, -0.5, None, ALU.mult))
                for _ in range(3):
                    own.settle(dve, dve.tensor_tensor(t, dst, dst, ALU.mult))
                    own.settle(dve, dve.tensor_tensor(t, t, v, ALU.mult))
                    own.settle(dve, dve.scalar_tensor_tensor(out=dst, in0=t, scalar=1.5, in1=dst, op0=ALU.add, op1=ALU.mult))

            def std_of(r, src, n):
                for t in range(n):
                    ins = dve.bn_stats(bst[:, t, :], src[:, t, :])
                own.settle(dve, ins)
                for t in range(n):
                    ins = dve.bn_aggr(mv[:, t, :], bst[:, t, :])
                own.settle(dve, ins)
                rsqrt(r[:, 0, :], mv[:, 0:n, 1], 1.0, n)
                return dve.scalar_tensor_tensor(out=r[:, 1, :], in0=mv[:, 0:n, 0], scalar=-1.0, in1=r[:, 0, :], op0=ALU.mult, op1=ALU.mult)

            def own_work_of_dve(name, b):
                if name == "stats_x":
                    dve.wait_ge(x_loaded[b], 16)
                    if b > 0:
                        dve.wait_ge(xn_ready, b)
                    own.settle(dve, std_of(r_x, X[:, b * BT:(b + 1) * BT, :], BT))
                    dve.engine_nop().then_inc(x_std, 1)
                elif name == "std_qk":
                    if b > 0:
                        dve.wait_ge(ks_ready, b)
                    rsqrt(r_qk[:, :, :].rearrange("p a t -> p (a t)"), ss_qk[:, :, :].rearrange("p a t -> p (a t)"), 1.0 / D, 2 * BT)
                    dve.engine_nop().then_inc(qk_std, 1)
                elif name == "residual":
                    rsqrt(r_p[:, :], ss_p[:, :], 1.0 / D, BT)
                    for t in range(BT):
                        T = b * BT + t
                        ins = dve.scalar_tensor_tensor(out=X[:, T, :], in0=proj[:, t, :], scalar=r_p[:, t:t + 1], in1=X[:, T, :],
                                                       op0=ALU.mult, op1=ALU.add)
                    own.settle(dve, ins)
                    if b > 0:
                        dve.wait_ge(xn2_ready, b)
                    own.settle(dve, std_of(r_n, X[:, b * BT:(b + 1) * BT, :], BT))
                    dve.engine_nop().then_inc(n_std, 1)

            def centre(dst, src, i, width=P):
                own.settle(dve, dve.tensor_reduce(wsum[:, i:i + 1], src, AX.X, ALU.add))
                own.settle(dve, dve.tensor_scalar(wsum[:, i:i + 1], wsum[:, i:i + 1], -1.0 / P, None, ALU.mult))
                ins = dve.tensor_scalar(dst, src, wsum[:, i:i + 1], None, ALU.add)
                return ins

            def dve_step(s):
                kind, b, g = s
                W = bank(s)
                if "V" not in READERS[kind]:
                    return
                dve.wait_ge(step_done, number[s] + 1)
                if "A" in READERS[kind]:
                    dve.wait_ge(act_drained, act_at[s])
                cols = slice(g * 512, (g + 1) * 512)
                if kind == "wa":
                    dve.wait_ge(row_loaded, 16 * 6)
                    own.settle(dve, centre(w_qkv[:, 0:P], W[:, 0:P], 0))
                    own.settle(dve, centre(w_qkv[:, P:2 * P], W[:, P:2 * P], 1))
                    ins = dve.tensor_tensor(scrap[:, 0, :], W[:, 3 * P:4 * P], b_row[:, 4, :], ALU.mult)
                    ins.then_inc(dve_drained, 1)
                    dve.wait_ge(dve_drained, dve_at[s])
                    own.settle(dve, centre(w_o[:, :], scrap[:, 0, :], 2))
                    own.settle(dve, centre(b_row[:, 0, :], b_row[:, 0, :], 3))
                    own.settle(dve, dve.tensor_tensor(b_row[:, 3, :], b_row[:, 3, :], b_row[:, 4, :], ALU.mult))
                    own.settle(dve, centre(b_row[:, 3, :], b_row[:, 3, :], 4))
                    own.settle(dve, centre(b_row[:, 1, :], b_row[:, 1, :], 5))
                    return
                if kind == "gt":
                    dve.tensor_copy(gate_T[:, :], W[:, 0:E])
                    dve.tensor_copy(bvT[:, :], W[:, P:2 * P]).then_inc(dve_drained, 1)
                    dve.wait_ge(dve_drained, dve_at[s])
                    dve.engine_nop().then_inc(weights_ready, 1)
                elif kind == "wv":
                    dve.tensor_copy(w_qkv[:, 2 * P:3 * P], W[:, 0:P])
                    dve.tensor_copy(b_row[:, 2, :], W[:, P:2 * P]).then_inc(dve_drained, 1)
                    dve.wait_ge(dve_drained, dve_at[s])
                    dve.engine_nop().then_inc(weights_ready, 1)
                elif kind == "qkv":
                    if g == 0 and b > 0:
                        dve.wait_ge(step_done, number[("kT", b - 1, 1)] + 1)
                        if b >= 2:
                            dve.wait_ge(pv_done, BT * (b - 1))
                    dve.tensor_tensor(QK[:, g, :, :], W[:, 0:2 * P].rearrange("p (a d) -> p a d", a=2), b_row[:, 0:2, :], ALU.add)
                    dve.tensor_tensor(V[:, b % 2, g, :], W[:, 2 * P:3 * P], b_row[:, 2, :], ALU.add).then_inc(dve_drained, 1)
                    dve.wait_ge(dve_drained, dve_at[s])
                    for a in range(2):
                        ins = dve.tensor_tensor_reduce(out=scrap[:, a, :], in0=QK[:, g, a, :], in1=QK[:, g, a, :], scale=1.0, scalar=0.0,
                                                       op0=ALU.mult, op1=ALU.add, accum_out=ss_qk[:, a, g:g + 1])
                    own.settle(dve, ins)
                elif kind == "qT":
                    dve.tensor_tensor(qT_lo[:, b % 2, cols], W, qT_hi[:, b % 2, cols].bitcast(F32), ALU.subtract
                                      ).then_inc(dve_drained, 1)
                elif kind == "kT":
                    dve.tensor_tensor(kT_lo[:, b % 2, cols], W, kT_hi[:, b % 2, cols].bitcast(F32), ALU.subtract
                                      ).then_inc(dve_drained, 1)
                elif kind == "wd":
                    dve.tensor_tensor(wdn_parts(b)[:, :, 1, :], W.rearrange("p (c h) -> p c h", h=D), wdn_parts(b)[:, :, 0, :].bitcast(F32),
                                      ALU.subtract).then_inc(dve_drained, 1)
                elif kind == "wu":
                    e = slice(b * I, (b + 1) * I)
                    dve.tensor_tensor(wup_lo[:, e], W, wup_hi[:, e].bitcast(F32), ALU.subtract).then_inc(dve_drained, 1)
                elif kind == "pj":
                    bias = b_row[:, 3:4, :].to_broadcast([P, GT, D])
                    ins = dve.tensor_tensor(proj[:, g * GT:(g + 1) * GT, :], W.rearrange("p (t d) -> p t d", d=D), bias, ALU.add)
                    ins.then_inc(dve_drained, 1)
                    dve.wait_ge(dve_drained, dve_at[s])
                    for t in range(g * GT, (g + 1) * GT):
                        own.up(dve.tensor_tensor_reduce(out=scrap[:, t % GT, :], in0=proj[:, t, :], in1=proj[:, t, :], scale=1.0, scalar=0.0,
                                                       op0=ALU.mult, op1=ALU.add, accum_out=ss_p[:, t:t + 1]))
                    dve.wait_ge(own.sem, own.n)
                elif kind == "lg":
                    bias = eb_row[:, :].unsqueeze(1).to_broadcast([P, BT, E])
                    ins = dve.tensor_tensor(L[:, b * BT:(b + 1) * BT, :], W[:, 0:BT * E].rearrange("p (t e) -> p t e", e=E), bias, ALU.add)
                    ins.then_inc(dve_drained, 1)
                    dve.wait_ge(dve_drained, dve_at[s])
                elif kind == "rt":
                    route_slots(b, W)
                    route_gates(b)

            def over_e(v):
                return v.unsqueeze(2).to_broadcast([P, HT, E])

            def over_t(v):
                return v.unsqueeze(1).to_broadcast([P, HT, E])

            def pick(src, best, one_hot):
                own.settle(dve, dve.tensor_reduce(best, src, AX.X, ALU.max))
                own.settle(dve, dve.tensor_tensor(rb[:, :, :], src, over_e(best), ALU.is_equal))
                own.settle(dve, dve.tensor_tensor(rb[:, :, :], rb[:, :, :], over_t(desc[:, :]), ALU.mult))
                own.settle(dve, dve.tensor_reduce(kk[:, :], rb[:, :, :], AX.X, ALU.max))
                own.settle(dve, dve.tensor_tensor(one_hot, over_e(kk[:, :]), over_t(desc[:, :]), ALU.is_equal))

            def route_choose(h):
                Lh = L[:, h * HT:(h + 1) * HT, :]
                if h == 0:
                    dve.wait_ge(consts, 6)
                pick(Lh, m1[:, :], oh[0][:, :, :])
                own.settle(dve, dve.tensor_copy(rec[:, h * HT:(h + 1) * HT, D + 1:D + 2], kk[:, :].unsqueeze(2)))
                own.settle(dve, dve.scalar_tensor_tensor(out=ra[:, :, :], in0=oh[0][:, :, :], scalar=-3.0e38, in1=Lh, op0=ALU.mult, op1=ALU.add))
                pick(ra[:, :, :], m2[:, :], oh[1][:, :, :])
                own.settle(dve, dve.tensor_tensor(ED[:, :, 0:E], Lh, over_e(m1[:, :]), ALU.subtract))
                own.settle(dve, dve.tensor_tensor(ED[:, :, E:E + 1], m2[:, :].unsqueeze(2), m1[:, :].unsqueeze(2), ALU.subtract))
                dve.engine_nop().then_inc(exp_in, 1)
                own.settle(dve, dve.tensor_tensor(chosen[:, :, :], oh[0][:, :, :], oh[1][:, :, :], ALU.add))
                dve.engine_nop().then_inc(chosen_ready, 1)

            def route_gates(h):
                dve.wait_ge(exp_out, h + 1)
                own.settle(dve, dve.tensor_reduce(zs[:, :], ED[:, :, 0:E], AX.X, ALU.add))
                own.settle(dve, dve.tensor_scalar(zs[:, :], zs[:, :], GATE_EPS, 1.0, ALU.mult, ALU.add))
                own.settle(dve, dve.tensor_tensor(zs[:, :], zs[:, :], ED[:, :, E], ALU.add))
                own.settle(dve, dve.reciprocal(gates[:, h, 0, :], zs[:, :]))
                own.settle(dve, dve.tensor_tensor(gates[:, h, 1, :], gates[:, h, 0, :], ED[:, :, E], ALU.mult))

            def route_slots(h, W):
                n = HT * E
                own.settle(dve, dve.tensor_copy(ra[:, :, :], W[:, 0:n].rearrange("p (t e) -> p t e", e=E)))
                ins = dve.tensor_copy(tot[:, :, :], W[:, n:2 * n].rearrange("p (t e) -> p e t", e=E))
                ins.then_inc(dve_drained, 1)
                dve.wait_ge(dve_drained, dve_at[("rt", h, 0)])
                flat = [v[:, :, :].rearrange("p e t -> p (e t)") for v in (incl, tot)]
                own.settle(dve, dve.tensor_tensor_scan(flat[0], seg[:, :], flat[1], 0.0, ALU.mult, ALU.add))
                count = incl[:, :, HT - 1:HT].to_broadcast([P, E, HT])
                own.settle(dve, dve.tensor_tensor(gtt[:, :, :], count, thr[:, :].unsqueeze(1).to_broadcast([P, E, HT]), ALU.is_gt))
                own.settle(dve, dve.tensor_reduce(ntile[:, :], gtt[:, :, :], AX.X, ALU.add))
                own.settle(dve, dve.tensor_tensor_scan(endt[:, :], ones[:, 0:E], ntile[:, :], 0.0, ALU.mult, ALU.add))
                own.settle(dve, dve.tensor_tensor(base[:, :], endt[:, :], ntile[:, :], ALU.subtract))
                own.settle(dve, dve.tensor_scalar(base[:, :], base[:, :], float(P), None, ALU.mult))
                own.settle(dve, dve.tensor_tensor(ext[:, :, :], endt[:, :].unsqueeze(1).to_broadcast([P, FT, E]),
                                                  tix[:, :].unsqueeze(2).to_broadcast([P, FT, E]), ALU.is_le))
                own.settle(dve, dve.tensor_reduce(exf[:, :], ext[:, :, :], AX.X, ALU.add))
                own.settle(dve, dve.tensor_scalar(exf[:, :], exf[:, :], float(E - 1), None, ALU.min))
                own.settle(dve, dve.tensor_copy(exp_packed[:, :], exf[:, :]))
                own.settle(dve, dve.tensor_scalar(tile_first[:, h, :], exf[:, :], -1.0, float(E), ALU.mult, ALU.add))
                for u in range(1, PACK):
                    own.settle(dve, dve.scalar_tensor_tensor(out=exp_packed[:, 0:FT - u], in0=exf[:, u:FT], scalar=float(E ** u),
                                                             in1=exp_packed[:, 0:FT - u], op0=ALU.mult, op1=ALU.add))
                own.settle(dve, dve.tensor_copy(experts[:, h, :], exp_packed[:, :]))
                own.settle(dve, dve.tensor_tensor(incl[:, :, :], incl[:, :, :], tot[:, :, :], ALU.subtract))
                own.settle(dve, dve.tensor_tensor(ra[:, :, :], ra[:, :, :], incl[:, :, :].rearrange("p e t -> p t e"), ALU.add))
                own.settle(dve, dve.tensor_tensor(ra[:, :, :], ra[:, :, :], over_t(base[:, :]), ALU.add))
                for k in range(TOPK):
                    own.settle(dve, dve.tensor_tensor(rb[:, :, :], ra[:, :, :], oh[k][:, :, :], ALU.mult))
                    own.settle(dve, dve.tensor_reduce(slots_f[:, :], rb[:, :, :], AX.X, ALU.add))
                    own.settle(dve, dve.tensor_copy(slots[:, h, k, :], slots_f[:, :]))
                dve.engine_nop().then_inc(routed, 1)

            def expert_step(h, i, k=0):
                t, k4 = h * FT + i, UNROLL * k
                if i + 2 < FT:
                    dve.wait_ge(xhi_ready, k4 + t + 3)
                    dve.tensor_tensor(xT_lo[:, t % 2, :], psX, xT_hi[:, t % 2, :].bitcast(F32), ALU.subtract).then_inc(xlo_ready, 1)
                if 0 <= i - 3:
                    dve.wait_ge(down_done, k4 + t - 2)
                    if t - 3 >= 4:
                        dve.wait_ge(y_scattered[(t - 3) % 4], 16 * k + 16 * ((t - 3) // 4))
                    dve.tensor_reduce(yo[:, (t - 3) % 4, :], psY.rearrange("p (a d) -> p d a", a=2), AX.X, ALU.add).then_inc(yo_ready, 1)
                if 0 <= i - 1 < FT:
                    par = (t - 1) % 2
                    dve.wait_ge(hhi_ready, k4 + t)
                    dve.tensor_tensor(hT_lo[:, par, :], psH[:, par, :], hT_hi[:, par, :].bitcast(F32), ALU.subtract).then_inc(hlo_ready, 1)

            def first_tiles(h):
                for i in range(-2, 0):
                    expert_step(h, i)

            def find_rows(h):
                dve.wait_ge(goes_loaded, 16 * (h + 1))
                own.settle(dve, dve.tensor_tensor(rows_f[:, :], goes_to[:, :, 1], tile_first[:, h, :], ALU.not_equal))
                own.settle(dve, dve.tensor_tensor(rows_f[:, :], rows_f[:, :], goes_to[:, :, 0], ALU.add))
                own.settle(dve, dve.scalar_tensor_tensor(out=goes_to[:, :, 1], in0=goes_to[:, :, 1], scalar=0.0, in1=tix[:, :],
                                                         op0=ALU.is_equal, op1=ALU.mult))
                own.settle(dve, dve.scalar_tensor_tensor(out=rows[:, h, :], in0=goes_to[:, :, 1], scalar=float(TOPK * P), in1=rows_f[:, :],
                                                         op0=ALU.mult, op1=ALU.add))
                dve.engine_nop().then_inc(rows_found, 1)

            ROWS_AT = 1
            def final_piece(kind, q):
                h, T0 = q * FP // HT, q * FP % HT
                if kind == "mix":
                    dve.wait_ge(mixed0, q + 1)
                    src = fo[q % 2]
                    for t in range(FP):
                        ins = dve.scalar_tensor_tensor(out=src[:, t, :], in0=two[q % 4][:, t, 1, :], scalar=gates[:, h, 1, T0 + t:T0 + t + 1],
                                                       in1=src[:, t, :], op0=ALU.mult, op1=ALU.add)
                    ins.then_inc(mixed, 1)
                    dve.wait_ge(mixed, q + 1)
                    if q >= 2:
                        dve.wait_ge(f_norm, q - 1)
                    own.settle(dve, std_of(r_of[0][q % 2], src, FP))
                    dve.engine_nop().then_inc(f_std, 1)
                elif kind == "stat2":
                    dve.wait_ge(f_added, q + 1)
                    if q >= 2:
                        dve.wait_ge(f_norm2, q - 1)
                    own.settle(dve, std_of(r_of[1][q % 2], fz[q % 4], FP))
                    dve.engine_nop().then_inc(f_std2, 1)

            for what, J, s in plan:
                if what == "own":
                    own_work_of_dve(*J)
                elif what in ("step", "setup"):
                    dve_step(s)
                    if s[0] == "lg" and (s[1] + 1) % HB == 0:
                        route_choose(s[1] // HB)
                elif what == "expert":
                    if J == 0:
                        first_tiles(0)
                    expert_step(0, J)
                    if J == ROWS_AT:
                        find_rows(0)

            for h in range(HALVES):
                if h > 0:
                    first_tiles(h)
                    for i in range(PEEL[h]):
                        expert_step(h, i)
                        if i == ROWS_AT:
                            find_rows(h)
                        for piece in final_beside.get(i, []):
                            final_piece(*piece)
                with dve.Fori(0, LOOPS[h]) as k:
                    for u in range(UNROLL):
                        expert_step(h, PEEL[h] + u, k)
                for i in range(PEEL[h] + UNROLL * LOOPS[h], STEPS):
                    expert_step(h, i)
            for piece in final_after:
                final_piece(*piece)


_INS = ['L0_attn_x', 'L0_attn_Wq', 'L0_attn_bq', 'L0_attn_Wk', 'L0_attn_bk', 'L0_attn_Wv', 'L0_attn_bv', 'L0_attn_Wo',
        'L0_attn_bo', 'L0_attn_layerscale', 'L0_ffn_gate_w', 'L0_ffn_expert_bias', 'L0_ffn_w_up', 'L0_ffn_w_down']


def kernel(**inputs):
    import numpy as _np
    import concourse.bacc as _bacc
    from concourse import mybir as _mybir
    from concourse.bass_utils import run_bass_kernel_spmd as _run

    nc = _bacc.Bacc("TRN2", target_bir_lowering=False, num_devices=1)
    arrays, args = {}, []
    for name in _INS:
        a = _np.ascontiguousarray(inputs[name])
        arrays[f"in_{name}_dram"] = a
        args.append(nc.dram_tensor(f"in_{name}_dram", a.shape, _mybir.dt.from_np(a.dtype), kind="ExternalInput").ap())
    shape = inputs['L0_attn_x'].shape
    args.append(nc.dram_tensor("out_0_dram", shape, _mybir.dt.float32, kind="ExternalOutput").ap())
    build_program(nc, *args)
    r = _run(nc, [arrays], core_ids=[0])
    return r.results[0]["out_0_dram"]
```

```python
from contextlib import ExitStack

import numpy as np

import concourse.bass as bass
from concourse import mybir

F32 = mybir.dt.float32
F32R = mybir.dt.float32r
I32 = mybir.dt.int32
U32 = mybir.dt.uint32
ALU = mybir.AluOpType
ACT = mybir.ActivationFunctionType
AX = mybir.AxisListType

P = 128
LN_EPS = 1e-5
GATE_EPS = 1e-6


class Count:

    def __init__(self, sem):
        self.sem, self.n = sem, 0

    def up(self, ins):
        self.n += 1
        ins.then_inc(self.sem, 1)

    def settle(self, eng, ins):
        self.up(ins)
        eng.wait_ge(self.sem, self.n)


def build_program(nc, x, Wq, bq, Wk, bk, Wv, bv, Wo, bo, layerscale, gate_w, expert_bias, w_up, w_down, out):
    B, S, D = x.shape
    E, I, _ = w_up.shape
    assert D == P and S % 512 == 0 and I == 512
    BT = S // P
    NT = B * BT
    HALVES = 2
    HT = NT // HALVES
    HB = B // HALVES
    TOPK = 2
    FT = (HT * P * TOPK + E * (P - 1)) // P
    TILES = HALVES * FT
    STEPS = TILES + 3
    UNROLL = 4
    PEEL = 21
    LOOP = (FT - 6 - PEEL) // UNROLL - 1
    AFTER = PEEL + UNROLL * LOOP
    BESIDE = FT + 8
    LATE = AFTER - 3
    ROUTED_AT = 15
    ROWS_AT = 1
    PACK = UNROLL + 3
    IC = I // P
    QG = S // 512
    GT = 512 // P
    LOG_S = float(np.log(np.float32(S)))
    K_SCALE = float(1.0 / np.sqrt(np.float32(D)))

    REC = D + 2
    xs = [nc.dram_tensor(f"sorted_x{h}", [FT * P, REC], F32, kind="Internal").ap() for h in range(HALVES)]
    zs_dram = [nc.dram_tensor(f"results{h}", [TOPK * (HT + FT) * P, D], F32, kind="Internal").ap() for h in range(HALVES)]

    x_t = x.rearrange("b (t p) d -> p (b t) d", p=P)
    out_t = out.rearrange("b (t p) d -> p (b t) d", p=P)

    with ExitStack() as ctx:
        def sb(name, shape, dt=F32):
            return ctx.enter_context(nc.sbuf_tensor(name, shape, dt))

        def sem(name):
            return ctx.enter_context(nc.semaphore(name))

        X = sb("X", [P, NT, D])
        rec = sb("rec", [P, NT, REC])
        XN2 = rec[:, :, 0:D]
        wup_hi = sb("wup_hi", [P, E * I], F32R)
        wup_lo = sb("wup_lo", [P, E * I], F32R)
        wdn = sb("wdn", [P, E * IC * 2 * D], F32R)
        stage_up = sb("stage_up", [P, 2, IC, P])
        stage_dn = sb("stage_dn", [P, 2, I])
        wnat = sb("wnat", [P, 4, P])
        w_half = sb("w_half", [P, 3 * P])
        w_qkv = sb("w_qkv", [P, 3 * P])
        w_o = sb("w_o", [P, P])
        b_col = sb("b_col", [P, 5])
        b_row = sb("b_row", [P, 4, P])
        gate_nat = sb("gate_nat", [E, P])
        gate_T = sb("gate_T", [P, E])
        eb_row = sb("eb_row", [P, E])
        ident = sb("ident", [P, P])
        ones = sb("ones", [P, P])
        centre = sb("centre", [P, P])
        centre_ls = sb("centre_ls", [P, P])
        before = sb("before", [P, P])
        no_token = sb("no_token", [P, 1, REC])
        neg_log_s = sb("neg_log_s", [P, 1])
        xT = sb("xT", [P, S])
        kT_hi = sb("kT_hi", [P, 2, S], F32R)
        kT_lo = sb("kT_lo", [P, 2, S], F32R)
        qT_hi = sb("qT_hi", [P, 2, S], F32R)
        qT_lo = sb("qT_lo", [P, 2, S], F32R)
        QK = sb("QK", [P, BT, 2, P])
        V = sb("V", [P, 2, BT, D])
        probs = sb("probs", [P, 2, S])
        oT = sb("oT", [P, S])
        proj = sb("proj", [P, BT, D])
        xn2T = sb("xn2T", [P, S])
        scrap = sb("scrap", [P, GT, P])
        L = sb("L", [P, NT, E])
        bst = sb("bst", [P, 2 * BT, 6])
        mv = sb("mv", [P, 2 * BT, 2])
        ss = sb("ss", [P, 3, BT])
        r_nx = sb("r_nx", [P, 2, 2 * BT])
        r_k = sb("r_k", [P, 2, BT])
        r_f = sb("r_f", [P, 2, 2, BT])
        eps = sb("eps", [P, 1])
        std_f = sb("std_f", [P, BT])
        r_qkp = sb("r_qkp", [P, 3, BT])
        nv, ntm = (sb(n, [P, 3 * BT]) for n in ("newton_v", "newton_t"))
        desc = sb("desc", [P, E])
        seg = sb("seg", [P, E * HT])
        thr = sb("thr", [P, HT])
        tix = sb("tix", [P, FT])
        m1 = sb("m1", [P, HT])
        m2 = sb("m2", [P, HT])
        kk = sb("kk", [P, HT])
        oh = [sb(f"oh{k}", [P, HT, E]) for k in range(TOPK)]
        ra = sb("ra", [P, HT, E])
        rb = sb("rb", [P, HT, E])
        ED = sb("ED", [P, HT, E + 1])
        zs = sb("zs", [P, HT])
        chosen = sb("chosen", [P, HT, E])
        incl = sb("incl", [P, E, HT])
        tot = sb("tot", [P, E, HT])
        gtt = sb("gtt", [P, E, HT])
        ntile = sb("ntile", [P, E])
        endt = sb("endt", [P, E])
        base = sb("base", [P, E])
        ext = sb("ext", [P, FT, E])
        exf = sb("exf", [P, FT])
        exp_packed = sb("exp_packed", [P, FT])
        experts = sb("experts", [P, HALVES, FT], I32)
        gates = sb("gates", [P, HALVES, TOPK, HT])
        slots_f = sb("slots_f", [P, HT])
        slots = sb("slots", [P, HALVES, TOPK, HT], U32)
        tile_first = sb("tile_first", [P, HALVES, FT])
        goes_to = sb("goes_to", [P, FT, 2])
        rows_f = sb("rows_f", [P, FT])
        rows = sb("rows", [P, HALVES, FT], U32)
        xin = sb("xin", [P, 4, D])
        xT_hi = sb("xT_hi", [P, 2, P], F32R)
        xT_lo = sb("xT_lo", [P, 2, P], F32R)
        hid = probs[:, 0, :].rearrange("p (a i) -> p a i", a=2)
        hT_hi = kT_hi[:, 0, :].rearrange("p (a i) -> p a i", a=2)
        hT_lo = kT_lo[:, 0, :].rearrange("p (a i) -> p a i", a=2)
        yo = sb("yo", [P, 4, D])
        yo_late = QK[:, :, :, :].rearrange("p t a d -> p (t a) d")
        FP = BT // 2
        PARTS = NT // FP
        DVE_ADDS = PARTS // 2
        v_flat = V[:, :, :, :].rearrange("p a t d -> p (a t d)").rearrange("p (t k d) -> p t k d", k=TOPK, d=D)
        two = [buf[:, a * FP:(a + 1) * FP, :, :] for buf in (QK, v_flat) for a in range(2)]
        fo = [proj[:, a * FP:(a + 1) * FP, :] for a in range(2)]
        oT_flat = oT[:, :].rearrange("p (t d) -> p t d", d=D)
        xn2T_flat = xn2T[:, :].rearrange("p (t d) -> p t d", d=D)
        fz = [buf[:, a * FP:(a + 1) * FP, :] for buf in (oT_flat, xn2T_flat) for a in range(2)]

        psS = ctx.enter_context(nc.psum_tensor("psS", [P, 2, S], F32))
        psO = ctx.enter_context(nc.psum_tensor("psO", [P, S], F32))
        psW = ctx.enter_context(nc.psum_tensor("psW", [P, 2, 512], F32))
        psU = psS[:, 0, :].rearrange("p (a n) -> p a n", a=2)
        psH = psS[:, 1, :].rearrange("p (a n) -> p a n", a=2)
        psX = psO[:, 0:P]
        psY = psO[:, 512:512 + 2 * D]

        x_loaded = [sem(f"x_loaded{b}") for b in range(B)]
        w_loaded = sem("w_loaded")
        row_loaded = sem("row_loaded")
        gate_loaded = sem("gate_loaded")
        scale_loaded = sem("scale_loaded")
        squares = sem("squares")
        up_loaded = [sem(f"up_loaded{i}") for i in range(2)]
        dn_loaded = [sem(f"dn_loaded{i}") for i in range(2)]
        cleared = sem("cleared")
        consts = sem("consts")
        weights_ready = sem("weights_ready")
        step_done = sem("step_done")
        act_drained = sem("act_drained")
        dve_drained = sem("dve_drained")
        scores_done = sem("scores_done")
        probs_ready = sem("probs_ready")
        pv_done = sem("pv_done")
        oT_ready = sem("oT_ready")
        qk_std = sem("qk_std")
        n_std = sem("n_std")
        qs_ready = sem("qs_ready")
        xn2_ready = sem("xn2_ready")
        exp_in = sem("exp_in")
        exp_out = sem("exp_out")
        chosen_ready = sem("chosen_ready")
        routed = sem("routed")
        experts_ready = sem("experts_ready")
        scattered = [sem(f"scattered{h}") for h in range(HALVES)]
        xin_loaded = [sem(f"xin_loaded{i}") for i in range(4)]
        xT_done = sem("xT_done")
        xhi_ready = sem("xhi_ready")
        xlo_ready = sem("xlo_ready")
        up_done = sem("up_done")
        hid_ready = sem("hid_ready")
        hT_done = sem("hT_done")
        hhi_ready = sem("hhi_ready")
        hlo_ready = sem("hlo_ready")
        down_done = sem("down_done")
        yo_ready = sem("yo_ready")
        goes_loaded = sem("goes_loaded")
        rows_found = sem("rows_found")
        y_scattered = [sem(f"y_scattered{i}") for i in range(4)]
        late_scattered = sem("late_scattered")
        z_loaded = [sem(f"z_loaded{q}") for q in range(PARTS)]
        weighted = sem("weighted")
        mixed = sem("mixed")
        f_var = sem("f_var")
        f_root = sem("f_root")
        f_added = sem("f_added")
        f_std2 = sem("f_std2")
        f_norm2 = sem("f_norm2")
        final_ready = sem("final_ready")
        stored = [sem(f"stored{q}") for q in range(PARTS)]
        s_dve, s_pool = sem("dve_own"), sem("pool_own")

        def front(b):
            return {1: [("qkv", b, t) for t in range(3, 6)], 2: [("qkv", b, t) for t in range(6, BT)],
                    3: [("kT", b, 0), ("kT", b, 1)], 4: [("qT", b, 0), ("qT", b, 1)]}

        def back(b):
            later = int(b == B - 2)
            early = int(b == HB - 1)
            return {1 + later: [("pj", b, 0)], 2 + later: [("pj", b, 1)], 7 - early: [("nT", b, 0), ("nT", b, 1), ("lg", b, 0)]}

        def weights_of(J):
            b, j = divmod(J, BT)
            n = {0: 0, 1: 1, 5: 2, 6: 3}.get(j)
            return [] if n is None else [("wu" if n % 2 == 0 else "wd", 2 * b + n // 2, 0)]

        def own_work(b):
            later = int(b == B - 1)
            return {2 + later: [("std_qkp", b + 1)], 3 + later: [("scale_q", b + 1), ("residual", b - 1)], 4 + later: [("stats_n", b - 1)],
                    6 + later - int(b == HB): [("norm_n", b - 1)]}

        CHOOSE = ("choose_first", "choose_second", "choose_both")
        SLOTS = ("expert_bases", "token_places", "token_slots", "tile_experts", "pack_experts", "gates")
        plan = [("setup", -1, s) for s in (("wa", 0, 0), ("wv", 0, 0))] + [("own", ("stats_x", 0), None)]
        plan += [("setup", -1, s) for s in (("xT", 0, 0), ("xT", 0, 1), ("wb", 0, 0), ("wc", 0, 0))]
        plan += [("step", -1, ("qkv", 0, t)) for t in range(BT)]
        plan += [("own", ("std_qkp", 0), None)] + [("step", -1, s) for s in (("kT", 0, 0), ("kT", 0, 1))]
        plan += [("own", ("scale_q", 0), None)] + [("step", -1, s) for s in (("qT", 0, 0), ("qT", 0, 1), ("gt", 0, 0), ("xT", 1, 0), ("xT", 1, 1))]
        plan += [("own", ("stats_x", 1), None)]
        NJ = B * BT
        for J in range(NJ):
            b, j = divmod(J, BT)
            plan.append(("scores", J, None))
            if b > 0 and not (b == B - 1 and j == BT - 1):
                plan += [("step", J, st) for st in back(b - 1).get(j, [])]
            if b + 1 < B:
                plan += [("step", J, st) for st in front(b + 1).get(j, [])]
            plan += [("step", J, st) for st in weights_of(J)]
            plan += [("own", w, None) for w in own_work(b).get(j, [])]
            if j == BT - 1 and b + 2 < B:
                plan += [("step", J, ("xT", b + 2, g)) for g in range(QG)] + [("own", ("stats_x", b + 2), None)]
            if j == BT - 2 and b == HB:
                plan += [("own", (w, 0), None) for w in CHOOSE]
            if j == BT - 1 and b == HB:
                plan += [("step", J, ("rt", 0, 0))] + [("own", (w, 0), None) for w in SLOTS[:3]]
            if j == 0 and b == HB + 1:
                plan += [("own", (w, 0), None) for w in SLOTS[3:]]
            if J > 0:
                plan.append(("pv", J - 1, None))
            if j == 0 and b + 1 < B:
                plan += [("step", J, ("qkv", b + 1, t)) for t in range(3)]
        plan.append(("pv", NJ - 1, None))
        plan += [("step", NJ, s) for s in back(B - 2)[BT - 1]]
        plan += [("step", NJ, s) for s in (("pj", B - 1, 0), ("pj", B - 1, 1))]
        LAST = tuple(f"last_{n}" for n in range(10))
        work = {n: [("own", (name, B - 1), None)] for n, name in enumerate(LAST)}
        work[10] = [("step", NJ, ("nT", B - 1, 0)), ("step", NJ, ("nT", B - 1, 1))]
        work[11] = [("step", NJ, ("lg", B - 1, 0))]
        for n, name in enumerate(CHOOSE[:2] + SLOTS[:5] + CHOOSE[2:] + SLOTS[5:]):
            work.setdefault(11 + n, []).append(("own", (name, HALVES - 1), None))
        work[13].insert(0, ("step", NJ, ("rt", HALVES - 1, 0)))
        for i in range(PEEL):
            plan.append(("expert", i, None))
            plan += work.get(i, [])

        final_beside = {}
        for q in range(PARTS // 2):
            for n, kinds in {-3: ["mix a"], -2: ["mix b"], 0: ["stat"], 1: ["std a"], 2: ["std b"], 3: ["add"], 4: ["stat2"], 5: ["std2 a"],
                             6: ["std2 b"], 7: ["norm2 a"], 8: ["norm2 b"]}.items():
                final_beside.setdefault(BESIDE + 8 * q + n, []).extend([(kind, q) for kind in kinds])
        final_after = [("mix a", PARTS // 2), ("mix b", PARTS // 2)]
        for c in range(PARTS // 2, PARTS + 1):
            final_after += [(kind, q) for kind, q in (("mix a", c + 1), ("mix b", c + 1), ("add", c - 1)) if PARTS // 2 <= q < PARTS]
            final_after.append(("both_std", c))
            if PARTS // 2 <= c - 1 < PARTS:
                final_after += [("norm2 a", c - 1), ("norm2 b", c - 1)]

        READERS = {"wa": "A", "gt": "V", "wv": "A", "wb": "A", "wc": "A", "xT": "A", "qkv": "V", "qT": "AV", "kT": "AV", "pj": "V",
                   "nT": "A", "lg": "V", "wu": "AV", "wd": "AV", "rt": "V"}
        steps = [s for _, _, s in plan if s is not None]
        number = {s: n for n, s in enumerate(steps)}
        act_at, dve_at, na, nd = {}, {}, 0, 0
        for s in steps:
            na += "A" in READERS[s[0]]
            nd += "V" in READERS[s[0]]
            act_at[s], dve_at[s] = na, nd

        def bank(s):
            return psW[:, number[s] % 2, :]

        def wdn_parts(e):
            return wdn[:, 2 * e * I:2 * (e + 1) * I].rearrange("p (c a h) -> p c a h", a=2, h=D)

        def late(t):
            return LATE <= t < FT

        def outputs(t):
            return yo_late[:, t - LATE, :] if late(t) else yo[:, t % 4, :]

        def ring_uses(t):
            return len([u for u in range(t % 4, t, 4) if not late(u)])

        def columns_of_round(c):
            return (0 if c < PARTS else FP), (2 * FP if c > PARTS // 2 else FP)

        def r_first(q):
            return r_f[:, q % 2, :, 0:FP]

        def r_second(q):
            return r_f[:, (q + 1) % 2, :, FP:2 * FP]

        block = ctx.enter_context(nc.Block())

        @block.sync
        def _(sp):
            def load_column(i, r):
                return sp.dma_start(b_col[:, i:i + 1], r.rearrange("(d a) -> d a", a=1))

            load_column(4, layerscale).then_inc(scale_loaded, 16)
            for i, w in enumerate((Wq, Wk, Wv, Wo)):
                sp.dma_start(wnat[:, i, :], w).then_inc(w_loaded, 16)
            sp.dma_start(X[:, 0:BT, :], x_t[:, 0:BT, :]).then_inc(x_loaded[0], 16)
            for i, r in enumerate((bq, bk, bv, bo)):
                load_column(i, r).then_inc(row_loaded, 16)
            sp.dma_start(eb_row[:, :], expert_bias.rearrange("(a d) -> a d", a=1).to_broadcast([P, E])).then_inc(row_loaded, 16)
            sp.dma_start(gate_nat[:, :], gate_w).then_inc(gate_loaded, 16)
            for b in range(1, B):
                sp.dma_start(X[:, b * BT:(b + 1) * BT, :], x_t[:, b * BT:(b + 1) * BT, :]).then_inc(x_loaded[b], 16)
            sp.wait_ge(consts, 4)
            for h in range(HALVES):
                sp.dma_start(xs[h].rearrange("(r p) d -> p r d", p=P), no_token[:, :, :].to_broadcast([P, FT, REC])).then_inc(cleared, 16)
            for e in range(E):
                if e >= 2:
                    sp.wait_ge(step_done, number[("wd", e - 2, 0)] + 1)
                sp.dma_start(stage_up[:, e % 2, :, :], w_up[e].rearrange("(c p) h -> p c h", p=P)).then_inc(up_loaded[e % 2], 16)
                sp.dma_start(stage_dn[:, e % 2, :], w_down[e]).then_inc(dn_loaded[e % 2], 16)

            def load_results(q):
                h = q * FP // HT
                if q * FP % HT == 0:
                    sp.wait_ge(late_scattered, 16 * (FT - LATE))
                    for t in (range(LATE - 4, LATE) if h == 0 else range(TILES - 4, TILES)):
                        sp.wait_ge(y_scattered[t % 4], 16 * (ring_uses(t) + 1))
                if q >= 4:
                    sp.wait_ge(mixed, q - 3)
                t = q * FP % HT
                src = zs_dram[h][TOPK * t * P:TOPK * (t + FP) * P, :].rearrange("(t p k) d -> p t k d", p=P, k=TOPK)
                sp.dma_start(two[q % 4], src).then_inc(z_loaded[q], 16)

            def store_final(q):
                sp.wait_ge(final_ready, q + 1)
                sp.dma_start(out_t[:, q * FP:(q + 1) * FP, :], fz[q % 4]).then_inc(stored[q], 16)

            def load(t, k=0):
                h, i = divmod(t, FT)
                if i == 0:
                    sp.wait_ge(scattered[h], 16 * HT * TOPK)
                if t >= UNROLL:
                    sp.wait_ge(xT_done, UNROLL * k + t - UNROLL + 1)
                sp.dma_start(xin[:, t % 4, :], xs[h][bass.ds(UNROLL * P * k + i * P, P), 0:D]).then_inc(xin_loaded[t % 4], 16)
                if i == 3 and t < PEEL or i == 3 and h > 0:
                    if h > 0:
                        sp.wait_ge(rows_found, h)
                    sp.dma_start(goes_to[:, :, :], xs[h].rearrange("(r p) d -> p r d", p=P)[:, :, D:D + 2]).then_inc(goes_loaded, 16)

            for t in range(PEEL + 6):
                load(t)
            with sp.Fori(0, LOOP) as k:
                for u in range(UNROLL):
                    load(PEEL + 6 + u, k)
            for t in range(AFTER, STEPS):
                if t + 6 < TILES:
                    load(t + 6)
                if t == FT + 3:
                    for q in range(PARTS // 2):
                        load_results(q)
                for kind, q in final_beside.get(t - 1, []):
                    if kind == "norm2 b":
                        store_final(q)
            for q in range(PARTS // 2, PARTS):
                load_results(q)
            for q in range(PARTS // 2, PARTS):
                store_final(q)
            for q in range(PARTS):
                sp.wait_ge(stored[q], 16)

        @block.gpsimd
        def _(pool):
            own = Count(s_pool)
            own.settle(pool, pool.memset(ident[:, :], 0.0))
            own.settle(pool, pool.affine_select(out=ident[:, :], in_=ident[:, :], compare_op=ALU.not_equal, fill=1.0, base=0,
                                                pattern=[[-1, P]], channel_multiplier=1))
            pool.tensor_scalar(centre[:, :], ident[:, :], -1.0 / P, None, ALU.add).then_inc(consts, 1)
            own.settle(pool, pool.memset(no_token[:, :, :], 0.0))
            pool.iota(no_token[:, 0, D:D + 1], pattern=[[0, 1]], base=TOPK * HT * P, channel_multiplier=TOPK,
                      allow_small_or_imprecise_dtypes=True).then_inc(consts, 1)
            own.settle(pool, pool.memset(ones[:, :], 1.0))
            pool.affine_select(out=before[:, :], in_=ones[:, :], compare_op=ALU.is_gt, fill=0.0, base=0,
                               pattern=[[1, P]], channel_multiplier=-1).then_inc(consts, 1)
            pool.memset(eps[:, :], LN_EPS)
            pool.memset(neg_log_s[:, :], -LOG_S).then_inc(consts, 1)
            for e in range(E):
                pool.memset(desc[:, e:e + 1], float(E - e))
            pool.memset(seg[:, :], 1.0)
            own.settle(pool, pool.iota(tix[:, :], pattern=[[1, FT]], base=0, channel_multiplier=0, allow_small_or_imprecise_dtypes=True))
            own.settle(pool, pool.tensor_scalar(thr[:, :], tix[:, 0:HT], float(P), None, ALU.mult))
            pool.memset(seg[:, :].rearrange("p (e t) -> p e t", t=HT)[:, :, 0:1], 0.0).then_inc(consts, 1)

            own.settle(pool, pool.iota(slots_f[:, :], pattern=[[TOPK * P, HT]], base=0, channel_multiplier=TOPK,
                                       allow_small_or_imprecise_dtypes=True))
            for h in range(HALVES):
                own.up(pool.tensor_copy(rec[:, h * HT:(h + 1) * HT, D:D + 1], slots_f[:, :].unsqueeze(2)))
            pool.wait_ge(own.sem, own.n)
            pool.engine_nop().then_inc(consts, 1)

            def scatter(h, t):
                for c in range(TOPK):
                    pool.indirect_dma_start(xs[h][:, :], bass.IndirectOffsetOnAxis(ap=slots[:, h, c, t:t + 1], axis=0),
                                            rec[:, h * HT + t, :], None).then_inc(scattered[h], 16)

            def scatter_y(h, i):
                t = h * FT + i
                pool.wait_ge(yo_ready, t + 1)
                pool.indirect_dma_start(zs_dram[h][:, :], bass.IndirectOffsetOnAxis(ap=rows[:, h, i:i + 1], axis=0),
                                        outputs(t), None).then_inc(late_scattered if late(t) else y_scattered[t % 4], 16)

            pool.wait_ge(cleared, 16 * HALVES)
            pool.wait_ge(xn2_ready, QG * HB)
            pool.wait_ge(routed, 1)
            for t in range(HT):
                scatter(0, t)
            pool.wait_ge(rows_found, 1)
            turn = ROUTED_AT - 2
            done = 0
            for i in range(LATE):
                if i == turn:
                    pool.wait_ge(xn2_ready, QG * B)
                    pool.wait_ge(routed, HALVES)
                if i >= turn:
                    for t in range(done, min(HT, 2 + (i - turn))):
                        scatter(1, t)
                        done = t + 1
                scatter_y(0, i)
            for t in range(done, HT):
                scatter(1, t)
            for i in range(LATE, FT):
                scatter_y(0, i)
            pool.wait_ge(rows_found, 2)

            def final_piece(kind, q):
                T0, fin = q * FP, fz[q % 4]
                if kind == "mix b" and q != DVE_ADDS:
                    pool.wait_ge(weighted, q + 1)
                    if q >= 2:
                        pool.wait_ge(f_added, q - 1)
                    pool.tensor_tensor(fo[q % 2], two[q % 4][:, :, 0, :], two[q % 4][:, :, 1, :], ALU.add).then_inc(mixed, 1)
                elif kind == "norm2 b":
                    pool.wait_ge(f_norm2, q + 1)
                    pool.tensor_tensor(fin, fin, X[:, T0:T0 + FP, :], ALU.add).then_inc(final_ready, 1)

            for i in range(FT):
                scatter_y(1, i)
                for piece in final_beside.get(FT + i + 3, []):
                    final_piece(*piece)
            for piece in final_after:
                final_piece(*piece)

        @block.scalar
        def _(act):
            def act_step(s):
                kind, b, g = s
                W = bank(s)
                if kind == "qkv" and b == 0:
                    act.wait_ge(dve_drained, dve_at[s])
                    for a, unused in enumerate((proj[:, g, :], oT[:, g * P:(g + 1) * P])):
                        ins = act.activation(unused, QK[:, g, a, :], ACT.Square, accum_out=ss[:, a, g:g + 1])
                    ins.then_inc(squares, 1)
                if "A" not in READERS[kind]:
                    return
                act.wait_ge(step_done, number[s] + 1)
                cols = slice(g * 512, (g + 1) * 512)
                if kind == "wa":
                    act.activation(w_half[:, 0:2 * P], W[:, 0:2 * P], ACT.Copy)
                    act.activation(w_o[:, :], W[:, 2 * P:3 * P], ACT.Copy).then_inc(act_drained, 1)
                elif kind == "wv":
                    act.activation(w_half[:, 2 * P:3 * P], W[:, 0:P], ACT.Copy).then_inc(act_drained, 1)
                elif kind == "wb":
                    act.activation(b_row[:, :, :].rearrange("p a d -> p (a d)"), W[:, 0:4 * P], ACT.Copy).then_inc(act_drained, 1)
                elif kind == "wc":
                    act.activation(w_qkv[:, :], W[:, 0:3 * P], ACT.Copy).then_inc(act_drained, 1)
                elif kind == "xT":
                    act.activation(xT[:, cols], W, ACT.Copy).then_inc(act_drained, 1)
                elif kind == "qT":
                    act.activation(qT_hi[:, b % 2, cols], W, ACT.Copy).then_inc(act_drained, 1)
                elif kind == "kT":
                    act.activation(kT_hi[:, b % 2, cols], W, ACT.Copy).then_inc(act_drained, 1)
                elif kind == "nT":
                    act.activation(xn2T[:, cols], W, ACT.Copy).then_inc(act_drained, 1)
                elif kind == "wu":
                    act.activation(wup_hi[:, b * I:(b + 1) * I], W, ACT.Copy).then_inc(act_drained, 1)
                elif kind == "wd":
                    act.activation(wdn_parts(b)[:, :, 0, :], W.rearrange("p (c h) -> p c h", h=D), ACT.Copy).then_inc(act_drained, 1)

            EXP_AT = "gates"

            def route_exp(h):
                act.wait_ge(exp_in, h + 1)
                act.activation(ED[:, :, :], ED[:, :, :], ACT.Exp).then_inc(exp_out, 1)

            def own_work_of_act(name, b):
                if name == "scale_q" and b < B:
                    act.wait_ge(qk_std, b + 1)
                    for t in range(BT):
                        ins = act.activation(QK[:, t, 0, :], QK[:, t, 0, :], ACT.Copy, scale=r_qkp[:, 0, t:t + 1])
                        if t % GT == GT - 1:
                            ins.then_inc(qs_ready, 1)
                elif name == "norm_n" and b >= 0 or name in LAST[-2:]:
                    act.wait_ge(n_std, b + 1)
                    half = BT // 2
                    for t in {"norm_n": range(BT), LAST[-2]: range(half), LAST[-1]: range(half, BT)}[name]:
                        ins = act.activation(XN2[:, b * BT + t, :], X[:, b * BT + t, :], ACT.Identity, bias=r_nx[:, 1, t:t + 1],
                                             scale=r_nx[:, 0, t:t + 1])
                        if t % GT == GT - 1:
                            ins.then_inc(xn2_ready, 1)

            def expert_step(t, k=0):
                k4 = UNROLL * k
                if 0 <= t < TILES:
                    act.wait_ge(up_done, k4 + t + 1)
                    act.activation(hid[:, t % 2, :], psU[:, t % 2, :], ACT.Gelu).then_inc(hid_ready, 1)
                if t + 2 < TILES:
                    act.wait_ge(xT_done, k4 + t + 3)
                    act.activation(xT_hi[:, t % 2, :], psX, ACT.Copy).then_inc(xhi_ready, 1)
                if 0 <= t - 1 < TILES:
                    act.wait_ge(hT_done, k4 + t)
                    act.activation(hT_hi[:, (t - 1) % 2, :], psH[:, (t - 1) % 2, :], ACT.Copy).then_inc(hhi_ready, 1)

            def final_piece(kind, q):
                h, T0 = q * FP // HT, q * FP % HT
                half = range(FP // 2) if kind[-1] == "a" else range(FP // 2, FP)
                if kind in ("mix a", "mix b"):
                    act.wait_ge(z_loaded[q], 16)
                    for t in half:
                        for c in range(TOPK if q != DVE_ADDS else 1):
                            z = two[q % 4][:, t, c, :]
                            ins = act.activation(z, z, ACT.Copy, scale=gates[:, h, c, T0 + t:T0 + t + 1])
                    if kind == "mix b":
                        ins.then_inc(weighted, 1)
                elif kind in ("norm2 a", "norm2 b"):
                    act.wait_ge(f_std2, q + 1)
                    r = r_second(q)
                    for t in half:
                        ins = act.activation(fz[q % 4][:, t, :], fz[q % 4][:, t, :], ACT.Identity, bias=r[:, 1, t:t + 1], scale=r[:, 0, t:t + 1])
                    if kind == "norm2 b":
                        ins.then_inc(f_norm2, 1)
                elif kind == "both_std":
                    act.wait_ge(f_var, q - PARTS // 2 + 1)
                    lo, hi = columns_of_round(q)
                    act.activation(std_f[:, lo:hi], mv[:, lo:hi, 1], ACT.Sqrt, bias=eps[:, 0:1]).then_inc(f_root, 1)

            for what, J, s in plan:
                if what == "own":
                    if J[0] == EXP_AT:
                        route_exp(J[1])
                    else:
                        own_work_of_act(*J)
                elif what == "scores":
                    b, j = divmod(J, BT)
                    if J == 0:
                        act.wait_ge(consts, 4)
                        act.activation(std_f[:, 0:1], eps[:, 0:1], ACT.Sigmoid)
                    act.wait_ge(scores_done, J + 1)
                    if J >= 2:
                        act.wait_ge(pv_done, J - 1)
                    act.activation(probs[:, J % 2, :], psS[:, J % 2, :], ACT.Sigmoid, bias=neg_log_s[:, 0:1],
                                   scale=r_k[:, b % 2, j:j + 1]).then_inc(probs_ready, 1)
                elif what == "pv":
                    if J % BT == BT - 1:
                        act.wait_ge(pv_done, J + 1)
                        if J // BT > 0:
                            act.wait_ge(step_done, number[("pj", J // BT - 1, 1)] + 1)
                        act.activation(oT[:, :], psO[:, :], ACT.Copy).then_inc(oT_ready, 1)
                elif what == "expert":
                    if J == 0:
                        act.activation(std_f[:, 0:1], eps[:, 0:1], ACT.Gelu)
                        expert_step(-2)
                        expert_step(-1)
                    expert_step(J)
                else:
                    act_step(s)

            with act.Fori(0, LOOP) as k:
                for u in range(UNROLL):
                    expert_step(PEEL + u, k)
            for t in range(AFTER, STEPS):
                expert_step(t)
                for piece in final_beside.get(t, []):
                    final_piece(*piece)
            act.activation(std_f[:, 0:1], eps[:, 0:1], ACT.Sqrt)
            for piece in final_after:
                final_piece(*piece)

        @block.tensor
        def _(pe):
            pe.wait_ge(consts, 5)

            def split3(dst, lhs, rhs, start=True, stop=True):
                pe.matmul(dst, lhs[0], rhs[0], start=True, stop=False)
                pe.matmul(dst, lhs[0], rhs[1], start=False, stop=False)
                return pe.matmul(dst, lhs[1], rhs[0], start=False, stop=True)

            def pe_step(s):
                kind, b, g = s
                W = bank(s)
                if number[s] >= 2:
                    last = steps[number[s] - 2]
                    if "A" in READERS[last[0]]:
                        pe.wait_ge(act_drained, act_at[last])
                    if "V" in READERS[last[0]]:
                        pe.wait_ge(dve_drained, dve_at[last])
                cols = slice(g * 512, (g + 1) * 512)
                if kind == "wa":
                    pe.wait_ge(w_loaded, 16 * 4)
                    pe.wait_ge(weights_ready, 1)
                    for i, (w, c) in enumerate(((0, centre), (1, centre), (3, centre_ls))):
                        ins = pe.matmul(W[:, i * P:(i + 1) * P], wnat[:, w, :], c[:, :], start=True, stop=True)
                elif kind == "wv":
                    pe.wait_ge(act_drained, act_at[("wa", 0, 0)])
                    ins = pe.matmul(W[:, 0:P], wnat[:, 2, :], w_o[:, :], start=True, stop=True)
                elif kind == "wb":
                    pe.wait_ge(row_loaded, 16 * 5)
                    for i, c in enumerate((centre, centre, w_o, centre_ls)):
                        ins = pe.matmul(W[:, i * P:(i + 1) * P], b_col[:, i:i + 1].to_broadcast([P, P]), c[:, :], start=True, stop=True)
                elif kind == "wc":
                    pe.wait_ge(act_drained, act_at[("wv", 0, 0)])
                    ins = pe.matmul(W[:, 0:3 * P], centre[:, :], w_half[:, :], start=True, stop=True)
                elif kind == "gt":
                    pe.wait_ge(gate_loaded, 16)
                    ins = pe.transpose(W[:, 0:E], gate_nat[:, :], ident[0:E, 0:E])
                elif kind == "xT":
                    pe.wait_ge(x_loaded[b], 16)
                    for t in range(GT):
                        ins = pe.transpose(W[:, t * P:(t + 1) * P], X[:, b * BT + g * GT + t, :], ident[:, :])
                elif kind == "qkv":
                    if g == 0:
                        pe.wait_ge(act_drained, act_at[("xT", b, 1)])
                        if b == 0:
                            pe.wait_ge(act_drained, act_at[("wc", 0, 0)])
                    ins = pe.matmul(W[:, 0:3 * P], xT[:, g * P:(g + 1) * P], w_qkv[:, :], start=True, stop=True)
                elif kind in ("qT", "kT"):
                    if kind == "qT":
                        pe.wait_ge(qs_ready, QG * b + g + 1)
                    else:
                        pe.wait_ge(dve_drained, dve_at[("qkv", b, BT - 1)])
                    for t in range(GT):
                        ins = pe.transpose(W[:, t * P:(t + 1) * P], QK[:, g * GT + t, int(kind == "kT"), :], ident[:, :])
                elif kind == "pj":
                    pe.wait_ge(oT_ready, b + 1)
                    for t in range(GT):
                        tt = g * GT + t
                        ins = pe.transpose(W[:, t * P:(t + 1) * P], oT[:, tt * P:(tt + 1) * P], ident[:, :])
                elif kind == "nT":
                    pe.wait_ge(xn2_ready, QG * b + g + 1)
                    for t in range(GT):
                        ins = pe.transpose(W[:, t * P:(t + 1) * P], XN2[:, b * BT + g * GT + t, :], ident[:, :])
                elif kind == "lg":
                    pe.wait_ge(act_drained, act_at[("nT", b, 1)])
                    for t in range(BT):
                        ins = pe.matmul(W[:, t * E:(t + 1) * E], xn2T[:, t * P:(t + 1) * P], gate_T[:, :], start=True, stop=True)
                elif kind == "wu":
                    pe.wait_ge(up_loaded[b % 2], 16 * (b // 2 + 1))
                    for c in range(IC):
                        ins = pe.transpose(W[:, c * P:(c + 1) * P], stage_up[:, b % 2, c, :], ident[:, :])
                elif kind == "wd":
                    pe.wait_ge(dn_loaded[b % 2], 16 * (b // 2 + 1))
                    for c in range(IC):
                        ins = pe.transpose(W[:, c * P:(c + 1) * P], stage_dn[:, b % 2, c * P:(c + 1) * P], ident[:, :])
                elif kind == "rt":
                    pe.wait_ge(chosen_ready, b + 1)
                    m = chosen[:, :, :].rearrange("p t e -> p (t e)")
                    pe.matmul(W[:, 0:HT * E], before[:, :], m, start=True, stop=True)
                    ins = pe.matmul(W[:, HT * E:2 * HT * E], ones[:, :], m, start=True, stop=True)
                ins.then_inc(step_done, 1)

            def scores(J):
                b, j = divmod(J, BT)
                if j == 0:
                    pe.wait_ge(act_drained, act_at[("qT", b, 1)])
                    pe.wait_ge(dve_drained, dve_at[("qT", b, 1)])
                if J >= 2:
                    pe.wait_ge(probs_ready, J - 1)
                keys = slice(j * P, (j + 1) * P)
                for g in range(QG):
                    cols = slice(g * 512, (g + 1) * 512)
                    ins = split3(psS[:, J % 2, cols], (kT_hi[:, b % 2, keys], kT_lo[:, b % 2, keys]),
                                 (qT_hi[:, b % 2, cols], qT_lo[:, b % 2, cols]))
                ins.then_inc(scores_done, 1)

            def pv(J):
                b, j = divmod(J, BT)
                pe.wait_ge(probs_ready, J + 1)
                if j == 0 and b > 0:
                    pe.wait_ge(oT_ready, b)
                for g in range(QG):
                    cols = slice(g * 512, (g + 1) * 512)
                    ins = pe.matmul(psO[:, cols], V[:, b % 2, j, :], probs[:, J % 2, cols], start=(j == 0), stop=(j == BT - 1))
                ins.then_inc(pv_done, 1)

            def turn_x(t, k, loads):
                pe.wait_ge(xin_loaded[t % 4], 16 * k + loads)
                if t > 0:
                    pe.wait_ge(xlo_ready, UNROLL * k + t)
                pe.transpose(psX, xin[:, t % 4, :], ident[:, :]).then_inc(xT_done, 1)

            def up(t, k, off):
                pe.wait_ge(xlo_ready, UNROLL * k + t + 1)
                dst, w = psU[:, t % 2, :], bass.ds(off, I)
                pe.matmul(dst, xT_hi[:, t % 2, :], wup_hi[:, w], start=True, stop=False)
                pe.matmul(dst, xT_hi[:, t % 2, :], wup_lo[:, w], start=False, stop=False)
                pe.matmul(dst, xT_lo[:, t % 2, :], wup_hi[:, w], start=False, stop=True).then_inc(up_done, 1)

            def turn_h(t, k):
                pe.wait_ge(hid_ready, UNROLL * k + t + 1)
                for c in range(IC):
                    ins = pe.transpose(psH[:, t % 2, c * P:(c + 1) * P], hid[:, t % 2, c * P:(c + 1) * P], ident[:, :])
                ins.then_inc(hT_done, 1)

            def down(t, k, off):
                pe.wait_ge(hlo_ready, UNROLL * k + t + 1)
                if t > 0:
                    pe.wait_ge(yo_ready, UNROLL * k + t)
                for c in range(IC):
                    w = wdn[:, bass.ds(off * 2 + c * 2 * D, 2 * D)]
                    pe.matmul(psY, hT_hi[:, t % 2, c * P:(c + 1) * P], w, start=(c == 0), stop=False)
                    ins = pe.matmul(psY, hT_lo[:, t % 2, c * P:(c + 1) * P], w, start=False, stop=(c == IC - 1))
                ins.then_inc(down_done, 1)

            def expert_step(t, k, offs):
                if 0 <= t < TILES:
                    up(t, k, offs[1])
                if t + 2 < TILES:
                    turn_x(t + 2, k, 16 * ((t + 2) // 4 + 1))
                if 0 <= t - 3:
                    down(t - 3, k, offs[0])
                if 0 <= t - 1 < TILES:
                    turn_h(t - 1, k)

            def offsets(h, i, n):
                packed = pe.value_load(experts[0:1, h, bass.ds(i, 1)], min_val=0, max_val=E ** PACK - 1)
                return [pe.snap(((packed >> (3 * u)) & (E - 1)) * I) for u in range(n)]

            known = {}

            def straight_step(t):
                for tile in (t - 3, t):
                    if 0 <= tile < TILES and tile not in known:
                        h, i = divmod(tile, FT)
                        if i == 0:
                            pe.wait_ge(experts_ready, h + 1)
                        for old in [o for o in known if o < t - 3]:
                            del known[old]
                        known.update(zip(range(tile, TILES), offsets(h, i, min(PACK, FT - i))))
                expert_step(t, 0, (known.get(t - 3), known.get(t)))

            for what, J, s in plan:
                if what == "scores":
                    scores(J)
                elif what == "pv":
                    pv(J)
                elif what == "expert":
                    if J == 0:
                        pe.wait_ge(oT_ready, B)
                        pe.wait_ge(probs_ready, NJ)
                        pe.wait_ge(act_drained, act_at[("wd", E - 1, 0)])
                        pe.wait_ge(dve_drained, dve_at[("wd", E - 1, 0)])
                        for t in range(-2, 0):
                            expert_step(t, 0, None)
                    straight_step(J)
                elif what != "own":
                    pe_step(s)

            with pe.Fori(0, LOOP) as k:
                offs = offsets(0, k * UNROLL + (PEEL - 3), PACK)
                for u in range(UNROLL):
                    expert_step(PEEL + u, k, (offs[u], offs[u + 3]))
            known.clear()
            for t in range(AFTER, STEPS):
                straight_step(t)

        @block.vector
        def _(dve):
            own = Count(s_dve)

            def rsqrt(dst, src, scale, n):
                rsqrt_start(dst, src, scale, n)
                newton(dst, n, 2)

            def rsqrt_start(dst, src, scale, n):
                v = nv[:, 0:n]
                own.settle(dve, dve.tensor_scalar(v, src, scale, LN_EPS, ALU.mult, ALU.add))
                own.settle(dve, dve.tensor_scalar(dst.bitcast(I32), v.bitcast(I32), -0.5, float(0x5f3759df), ALU.mult, ALU.add))
                own.settle(dve, dve.tensor_scalar(v, v, -0.5, None, ALU.mult))
                newton(dst, n, 1)

            def newton(dst, n, times):
                v, t = nv[:, 0:n], ntm[:, 0:n]
                for _ in range(times):
                    own.settle(dve, dve.tensor_tensor(t, dst, dst, ALU.mult))
                    own.settle(dve, dve.tensor_tensor(t, t, v, ALU.mult))
                    own.settle(dve, dve.scalar_tensor_tensor(out=dst, in0=t, scalar=1.5, in1=dst, op0=ALU.add, op1=ALU.mult))

            def stats_of(src, n, at=0):
                for t in range(n):
                    ins = dve.bn_stats(bst[:, at + t, :], src[:, t, :])
                own.settle(dve, ins)
                for t in range(n):
                    ins = dve.bn_aggr(mv[:, at + t, :], bst[:, at + t, :])
                own.settle(dve, ins)

            def std_of_stats(r, lo, hi):
                rsqrt_start(r[:, 0, :], mv[:, lo:hi, 1], 1.0, hi - lo)
                end_of_std(r, lo, hi)

            def end_of_std(r, lo, hi):
                newton(r[:, 0, :], hi - lo, 2)
                own.settle(dve, dve.scalar_tensor_tensor(out=r[:, 1, :], in0=mv[:, lo:hi, 0], scalar=-1.0, in1=r[:, 0, :], op0=ALU.mult, op1=ALU.mult))

            def own_work_of_dve(name, b):
                if name == "stats_x":
                    dve.wait_ge(x_loaded[b], 16)
                    stats_of(X[:, b * BT:(b + 1) * BT, :], BT, at=BT)
                    std_of_stats(r_nx[:, :, BT:2 * BT], BT, 2 * BT)
                elif name == "stats_n" and b >= 0:
                    stats_of(X[:, b * BT:(b + 1) * BT, :], BT)
                    if b > 0:
                        dve.wait_ge(xn2_ready, QG * b)
                    std_of_stats(r_nx[:, :, 0:BT], 0, BT)
                    dve.engine_nop().then_inc(n_std, 1)
                elif name == "std_qkp":
                    if 1 < b <= B:
                        dve.wait_ge(qs_ready, QG * b)
                    if b == 0:
                        dve.wait_ge(squares, BT)
                    lo, hi = (0 if b < B else 2), (3 if b >= 2 else 2)
                    r, v = (a[:, lo:hi, :].rearrange("p a t -> p (a t)") for a in (r_qkp, ss))
                    rsqrt(r, v, 1.0 / D, (hi - lo) * BT)
                    if b < B:
                        if b >= 2:
                            dve.wait_ge(probs_ready, BT * (b - 1))
                        own.settle(dve, dve.tensor_scalar(r_k[:, b % 2, :], r_qkp[:, 1, :], K_SCALE, None, ALU.mult))
                        dve.engine_nop().then_inc(qk_std, 1)
                elif name == "residual" and b >= 0:
                    for t in range(BT):
                        T = b * BT + t
                        ins = dve.scalar_tensor_tensor(out=X[:, T, :], in0=proj[:, t, :], scalar=r_qkp[:, 2, t:t + 1], in1=X[:, T, :],
                                                       op0=ALU.mult, op1=ALU.add)
                    own.settle(dve, ins)

            def last_batch(n):
                b, half = B - 1, BT // 2
                tiles = slice((n % 2) * half, (n % 2 + 1) * half)
                if n == 0:
                    rsqrt_start(r_qkp[:, 2, :], ss[:, 2, :], 1.0 / D, BT)
                elif n == 1:
                    newton(r_qkp[:, 2, :], BT, 2)
                elif n in (2, 3):
                    for t in range(BT)[tiles]:
                        ins = dve.scalar_tensor_tensor(out=X[:, b * BT + t, :], in0=proj[:, t, :], scalar=r_qkp[:, 2, t:t + 1],
                                                       in1=X[:, b * BT + t, :], op0=ALU.mult, op1=ALU.add)
                    own.settle(dve, ins)
                elif n in (4, 5):
                    stats_of(X[:, b * BT:(b + 1) * BT, :][:, tiles, :], half, at=tiles.start)
                elif n == 6:
                    dve.wait_ge(xn2_ready, QG * b)
                    rsqrt_start(r_nx[:, 0, 0:BT], mv[:, 0:BT, 1], 1.0, BT)
                elif n == 7:
                    end_of_std(r_nx[:, :, 0:BT], 0, BT)
                    dve.engine_nop().then_inc(n_std, 1)

            def centre_weights():
                dve.wait_ge(scale_loaded, 16)
                dve.wait_ge(consts, 1)
                own.settle(dve, dve.tensor_scalar(centre_ls[:, :], centre[:, :], b_col[:, 4:5], None, ALU.mult))
                dve.engine_nop().then_inc(weights_ready, 1)

            def dve_step(s):
                kind, b, g = s
                W = bank(s)
                if "V" not in READERS[kind]:
                    return
                dve.wait_ge(step_done, number[s] + 1)
                if "A" in READERS[kind]:
                    dve.wait_ge(act_drained, act_at[s])
                cols = slice(g * 512, (g + 1) * 512)
                if kind == "gt":
                    dve.tensor_copy(gate_T[:, :], W[:, 0:E]).then_inc(dve_drained, 1)
                elif kind == "qkv":
                    if g == 0 and b == 0:
                        dve.wait_ge(act_drained, act_at[("wb", 0, 0)])
                    if g == 0 and b > 0:
                        dve.wait_ge(step_done, number[("qT", b - 1, 1)] + 1)
                        if b >= 2:
                            dve.wait_ge(pv_done, BT * (b - 1))
                    r = r_nx[:, 0, BT + g:BT + g + 1]
                    dve.scalar_tensor_tensor(out=QK[:, g, :, :], in0=W[:, 0:2 * P].rearrange("p (a d) -> p a d", a=2), scalar=r,
                                             in1=b_row[:, 0:2, :], op0=ALU.mult, op1=ALU.add)
                    dve.scalar_tensor_tensor(out=V[:, b % 2, g, :], in0=W[:, 2 * P:3 * P], scalar=r, in1=b_row[:, 2, :],
                                             op0=ALU.mult, op1=ALU.add).then_inc(dve_drained, 1)
                    dve.wait_ge(dve_drained, dve_at[s])
                    for a in range(2) if b > 0 else []:
                        ins = dve.tensor_tensor_reduce(out=scrap[:, a, :], in0=QK[:, g, a, :], in1=QK[:, g, a, :], scale=1.0, scalar=0.0,
                                                       op0=ALU.mult, op1=ALU.add, accum_out=ss[:, a, g:g + 1])
                    if b > 0:
                        own.settle(dve, ins)
                elif kind == "qT":
                    dve.tensor_tensor(qT_lo[:, b % 2, cols], W, qT_hi[:, b % 2, cols].bitcast(F32), ALU.subtract
                                      ).then_inc(dve_drained, 1)
                elif kind == "kT":
                    dve.tensor_tensor(kT_lo[:, b % 2, cols], W, kT_hi[:, b % 2, cols].bitcast(F32), ALU.subtract
                                      ).then_inc(dve_drained, 1)
                elif kind == "wd":
                    dve.tensor_tensor(wdn_parts(b)[:, :, 1, :], W.rearrange("p (c h) -> p c h", h=D), wdn_parts(b)[:, :, 0, :].bitcast(F32),
                                      ALU.subtract).then_inc(dve_drained, 1)
                elif kind == "wu":
                    e = slice(b * I, (b + 1) * I)
                    dve.tensor_tensor(wup_lo[:, e], W, wup_hi[:, e].bitcast(F32), ALU.subtract).then_inc(dve_drained, 1)
                elif kind == "pj":
                    bias = b_row[:, 3:4, :].to_broadcast([P, GT, D])
                    ins = dve.tensor_tensor(proj[:, g * GT:(g + 1) * GT, :], W.rearrange("p (t d) -> p t d", d=D), bias, ALU.add)
                    ins.then_inc(dve_drained, 1)
                    dve.wait_ge(dve_drained, dve_at[s])
                    for t in range(g * GT, (g + 1) * GT):
                        own.up(dve.tensor_tensor_reduce(out=scrap[:, t % GT, :], in0=proj[:, t, :], in1=proj[:, t, :], scale=1.0, scalar=0.0,
                                                       op0=ALU.mult, op1=ALU.add, accum_out=ss[:, 2, t:t + 1]))
                    dve.wait_ge(own.sem, own.n)
                elif kind == "lg":
                    if b == 0:
                        dve.wait_ge(row_loaded, 16 * 5)
                    bias = eb_row[:, :].unsqueeze(1).to_broadcast([P, BT, E])
                    ins = dve.tensor_tensor(L[:, b * BT:(b + 1) * BT, :], W[:, 0:BT * E].rearrange("p (t e) -> p t e", e=E), bias, ALU.add)
                    ins.then_inc(dve_drained, 1)
                    dve.wait_ge(dve_drained, dve_at[s])
                elif kind == "rt":
                    n = HT * E
                    dve.tensor_copy(ra[:, :, :], W[:, 0:n].rearrange("p (t e) -> p t e", e=E))
                    dve.tensor_copy(tot[:, :, :], W[:, n:2 * n].rearrange("p (t e) -> p e t", e=E)).then_inc(dve_drained, 1)
                    dve.wait_ge(dve_drained, dve_at[s])

            def over_e(v):
                return v.unsqueeze(2).to_broadcast([P, HT, E])

            def over_t(v):
                return v.unsqueeze(1).to_broadcast([P, HT, E])

            def pick(src, best, one_hot):
                own.settle(dve, dve.tensor_reduce(best, src, AX.X, ALU.max))
                own.settle(dve, dve.tensor_tensor(rb[:, :, :], src, over_e(best), ALU.is_equal))
                own.settle(dve, dve.tensor_tensor(rb[:, :, :], rb[:, :, :], over_t(desc[:, :]), ALU.mult))
                own.settle(dve, dve.tensor_reduce(kk[:, :], rb[:, :, :], AX.X, ALU.max))
                own.settle(dve, dve.tensor_tensor(one_hot, over_e(kk[:, :]), over_t(desc[:, :]), ALU.is_equal))

            def route(name, h):
                Lh = L[:, h * HT:(h + 1) * HT, :]
                flat = [v[:, :, :].rearrange("p e t -> p (e t)") for v in (incl, tot)]
                if name == "choose_first":
                    if h == 0:
                        dve.wait_ge(consts, 6)
                    pick(Lh, m1[:, :], oh[0][:, :, :])
                    own.settle(dve, dve.tensor_copy(rec[:, h * HT:(h + 1) * HT, D + 1:D + 2], kk[:, :].unsqueeze(2)))
                elif name == "choose_second":
                    own.settle(dve, dve.scalar_tensor_tensor(out=ra[:, :, :], in0=oh[0][:, :, :], scalar=-3.0e38, in1=Lh, op0=ALU.mult, op1=ALU.add))
                    pick(ra[:, :, :], m2[:, :], oh[1][:, :, :])
                    own.settle(dve, dve.tensor_tensor(chosen[:, :, :], oh[0][:, :, :], oh[1][:, :, :], ALU.add))
                    dve.engine_nop().then_inc(chosen_ready, 1)
                elif name == "choose_both":
                    own.settle(dve, dve.tensor_tensor(ED[:, :, 0:E], Lh, over_e(m1[:, :]), ALU.subtract))
                    own.settle(dve, dve.tensor_tensor(ED[:, :, E:E + 1], m2[:, :].unsqueeze(2), m1[:, :].unsqueeze(2), ALU.subtract))
                    dve.engine_nop().then_inc(exp_in, 1)
                elif name == "expert_bases":
                    own.settle(dve, dve.tensor_tensor_scan(flat[0], seg[:, :], flat[1], 0.0, ALU.mult, ALU.add))
                    count = incl[:, :, HT - 1:HT].to_broadcast([P, E, HT])
                    own.settle(dve, dve.tensor_tensor(gtt[:, :, :], count, thr[:, :].unsqueeze(1).to_broadcast([P, E, HT]), ALU.is_gt))
                    own.settle(dve, dve.tensor_reduce(ntile[:, :], gtt[:, :, :], AX.X, ALU.add))
                    own.settle(dve, dve.tensor_tensor_scan(endt[:, :], ones[:, 0:E], ntile[:, :], 0.0, ALU.mult, ALU.add))
                    own.settle(dve, dve.tensor_tensor(base[:, :], endt[:, :], ntile[:, :], ALU.subtract))
                    own.settle(dve, dve.tensor_scalar(base[:, :], base[:, :], float(P), None, ALU.mult))
                elif name == "token_places":
                    own.settle(dve, dve.tensor_tensor(incl[:, :, :], incl[:, :, :], tot[:, :, :], ALU.subtract))
                    own.settle(dve, dve.tensor_tensor(ra[:, :, :], ra[:, :, :], incl[:, :, :].rearrange("p e t -> p t e"), ALU.add))
                    own.settle(dve, dve.tensor_tensor(ra[:, :, :], ra[:, :, :], over_t(base[:, :]), ALU.add))
                elif name == "token_slots":
                    for k in range(TOPK):
                        own.settle(dve, dve.tensor_tensor(rb[:, :, :], ra[:, :, :], oh[k][:, :, :], ALU.mult))
                        own.settle(dve, dve.tensor_reduce(slots_f[:, :], rb[:, :, :], AX.X, ALU.add))
                        own.settle(dve, dve.tensor_copy(slots[:, h, k, :], slots_f[:, :]))
                    dve.engine_nop().then_inc(routed, 1)
                elif name == "tile_experts":
                    own.settle(dve, dve.tensor_tensor(ext[:, :, :], endt[:, :].unsqueeze(1).to_broadcast([P, FT, E]),
                                                      tix[:, :].unsqueeze(2).to_broadcast([P, FT, E]), ALU.is_le))
                    own.settle(dve, dve.tensor_reduce(exf[:, :], ext[:, :, :], AX.X, ALU.add))
                    own.settle(dve, dve.tensor_scalar(exf[:, :], exf[:, :], float(E - 1), None, ALU.min))
                    own.settle(dve, dve.tensor_scalar(tile_first[:, h, :], exf[:, :], -1.0, float(E), ALU.mult, ALU.add))
                elif name == "pack_experts":
                    own.settle(dve, dve.tensor_copy(exp_packed[:, :], exf[:, :]))
                    for u in range(1, PACK):
                        own.settle(dve, dve.scalar_tensor_tensor(out=exp_packed[:, 0:FT - u], in0=exf[:, u:FT], scalar=float(E ** u),
                                                                 in1=exp_packed[:, 0:FT - u], op0=ALU.mult, op1=ALU.add))
                    own.settle(dve, dve.tensor_copy(experts[:, h, :], exp_packed[:, :]))
                    dve.engine_nop().then_inc(experts_ready, 1)
                elif name == "gates":
                    dve.wait_ge(exp_out, h + 1)
                    own.settle(dve, dve.tensor_reduce(zs[:, :], ED[:, :, 0:E], AX.X, ALU.add))
                    own.settle(dve, dve.tensor_scalar(zs[:, :], zs[:, :], GATE_EPS, 1.0, ALU.mult, ALU.add))
                    own.settle(dve, dve.tensor_tensor(zs[:, :], zs[:, :], ED[:, :, E], ALU.add))
                    own.settle(dve, dve.reciprocal(gates[:, h, 0, :], zs[:, :]))
                    own.settle(dve, dve.tensor_tensor(gates[:, h, 1, :], gates[:, h, 0, :], ED[:, :, E], ALU.mult))

            def expert_step(t, k=0):
                k4 = UNROLL * k
                if t + 2 < TILES:
                    dve.wait_ge(xhi_ready, k4 + t + 3)
                    dve.tensor_tensor(xT_lo[:, t % 2, :], psX, xT_hi[:, t % 2, :].bitcast(F32), ALU.subtract).then_inc(xlo_ready, 1)
                if 0 <= t - 3:
                    dve.wait_ge(down_done, k4 + t - 2)
                    if t - 3 >= 4 and not late(t - 3):
                        dve.wait_ge(y_scattered[(t - 3) % 4], 16 * k + 16 * ring_uses(t - 3))
                    dve.tensor_reduce(outputs(t - 3), psY.rearrange("p (a d) -> p d a", a=2), AX.X, ALU.add).then_inc(yo_ready, 1)
                if 0 <= t - 1 < TILES:
                    par = (t - 1) % 2
                    dve.wait_ge(hhi_ready, k4 + t)
                    dve.tensor_tensor(hT_lo[:, par, :], psH[:, par, :], hT_hi[:, par, :].bitcast(F32), ALU.subtract).then_inc(hlo_ready, 1)

            def find_rows(h):
                dve.wait_ge(goes_loaded, 16 * (h + 1))
                own.settle(dve, dve.tensor_tensor(rows_f[:, :], goes_to[:, :, 1], tile_first[:, h, :], ALU.not_equal))
                own.settle(dve, dve.tensor_tensor(rows_f[:, :], rows_f[:, :], goes_to[:, :, 0], ALU.add))
                own.settle(dve, dve.scalar_tensor_tensor(out=goes_to[:, :, 1], in0=goes_to[:, :, 1], scalar=0.0, in1=tix[:, :],
                                                         op0=ALU.is_equal, op1=ALU.mult))
                own.settle(dve, dve.scalar_tensor_tensor(out=rows[:, h, :], in0=goes_to[:, :, 1], scalar=float(TOPK * P), in1=rows_f[:, :],
                                                         op0=ALU.mult, op1=ALU.add))
                dve.engine_nop().then_inc(rows_found, 1)

            def final_piece(kind, q):
                h, T0 = q * FP // HT, q * FP % HT
                half = PARTS // 2
                if kind == "stat":
                    dve.wait_ge(mixed, q + 1)
                    stats_of(fo[q % 2], FP)
                elif kind == "add":
                    if q >= 4:
                        dve.wait_ge(stored[q - 4], 16)
                    for t in range(FP):
                        ins = dve.scalar_tensor_tensor(out=fz[q % 4][:, t, :], in0=fo[q % 2][:, t, :], scalar=r_first(q)[:, 0, t:t + 1],
                                                       in1=XN2[:, q * FP + t, :], op0=ALU.mult, op1=ALU.add)
                    ins.then_inc(f_added, 1)
                elif kind == "stat2":
                    dve.wait_ge(f_added, q + 1)
                    stats_of(fz[q % 4], FP, at=FP)
                elif kind == "std a":
                    rsqrt_start(r_first(q)[:, 0, :], mv[:, 0:FP, 1], 1.0, FP)
                elif kind == "std b":
                    end_of_std(r_first(q), 0, FP)
                elif kind == "std2 a":
                    if q >= 2:
                        dve.wait_ge(f_norm2, q - 1)
                    rsqrt_start(r_second(q)[:, 0, :], mv[:, FP:2 * FP, 1], 1.0, FP)
                elif kind == "std2 b":
                    end_of_std(r_second(q), FP, 2 * FP)
                    dve.engine_nop().then_inc(f_std2, 1)
                elif kind == "both_std":
                    lo, hi = columns_of_round(q)
                    if q == DVE_ADDS:
                        dve.wait_ge(weighted, q + 1)
                        dve.wait_ge(mixed, q)
                        for t in range(FP):
                            ins = dve.scalar_tensor_tensor(out=fo[q % 2][:, t, :], in0=two[q % 4][:, t, 1, :],
                                                           scalar=gates[:, h, 1, T0 + t:T0 + t + 1], in1=two[q % 4][:, t, 0, :],
                                                           op0=ALU.mult, op1=ALU.add)
                        own.settle(dve, ins)
                    elif q < PARTS:
                        dve.wait_ge(mixed, q)
                    if q < PARTS:
                        for t in range(FP):
                            ins = dve.bn_stats(bst[:, t, :], fo[q % 2][:, t, :])
                    if q > half:
                        dve.wait_ge(f_added, q)
                        for t in range(FP):
                            ins = dve.bn_stats(bst[:, FP + t, :], fz[(q - 1) % 4][:, t, :])
                    own.settle(dve, ins)
                    for t in range(lo, hi):
                        ins = dve.bn_aggr(mv[:, t, :], bst[:, t, :])
                    own.settle(dve, ins)
                    dve.engine_nop().then_inc(f_var, 1)
                    r, v, t = r_f[:, q % 2, :, lo:hi], nv[:, lo:hi], ntm[:, lo:hi]
                    own.settle(dve, dve.tensor_scalar(v, mv[:, lo:hi, 1], LN_EPS, -0.5, ALU.add, ALU.mult))
                    if q > half:
                        dve.wait_ge(f_norm2, q - 2)
                    dve.wait_ge(f_root, q - half + 1)
                    own.settle(dve, dve.reciprocal(r[:, 0, :], std_f[:, lo:hi]))
                    own.settle(dve, dve.tensor_tensor(t, r[:, 0, :], r[:, 0, :], ALU.mult))
                    own.settle(dve, dve.tensor_tensor(t, t, v, ALU.mult))
                    own.settle(dve, dve.scalar_tensor_tensor(out=r[:, 0, :], in0=t, scalar=1.5, in1=r[:, 0, :], op0=ALU.add, op1=ALU.mult))
                    own.settle(dve, dve.scalar_tensor_tensor(out=r[:, 1, :], in0=mv[:, lo:hi, 0], scalar=-1.0, in1=r[:, 0, :],
                                                             op0=ALU.mult, op1=ALU.mult))
                    if q > half:
                        dve.engine_nop().then_inc(f_std2, 1)

            centre_weights()
            for what, J, s in plan:
                if what == "own" and J[0] in LAST:
                    last_batch(LAST.index(J[0]))
                elif what == "own":
                    (route if J[0] in CHOOSE + SLOTS else own_work_of_dve)(*J)
                elif what in ("step", "setup"):
                    dve_step(s)
                elif what == "expert":
                    if J == 0:
                        expert_step(-2)
                        expert_step(-1)
                    expert_step(J)
                    if J == ROWS_AT:
                        find_rows(0)

            with dve.Fori(0, LOOP) as k:
                for u in range(UNROLL):
                    expert_step(PEEL + u, k)
            for t in range(AFTER, STEPS):
                expert_step(t)
                if t == FT + ROWS_AT:
                    find_rows(1)
                for piece in final_beside.get(t, []):
                    final_piece(*piece)
            for piece in final_after:
                final_piece(*piece)


_INS = ['L0_attn_x', 'L0_attn_Wq', 'L0_attn_bq', 'L0_attn_Wk', 'L0_attn_bk', 'L0_attn_Wv', 'L0_attn_bv', 'L0_attn_Wo',
        'L0_attn_bo', 'L0_attn_layerscale', 'L0_ffn_gate_w', 'L0_ffn_expert_bias', 'L0_ffn_w_up', 'L0_ffn_w_down']


def kernel(**inputs):
    import numpy as _np
    import concourse.bacc as _bacc
    from concourse import mybir as _mybir
    from concourse.bass_utils import run_bass_kernel_spmd as _run

    nc = _bacc.Bacc("TRN2", target_bir_lowering=False, num_devices=1)
    arrays, args = {}, []
    for name in _INS:
        a = _np.ascontiguousarray(inputs[name])
        arrays[f"in_{name}_dram"] = a
        args.append(nc.dram_tensor(f"in_{name}_dram", a.shape, _mybir.dt.from_np(a.dtype), kind="ExternalInput").ap())
    shape = inputs['L0_attn_x'].shape
    args.append(nc.dram_tensor("out_0_dram", shape, _mybir.dt.float32, kind="ExternalOutput").ap())
    build_program(nc, *args)
    r = _run(nc, [arrays], core_ids=[0])
    return r.results[0]["out_0_dram"]
```
